# Optimizing a Trainium2 kernel written in Bass

```python
import numpy as np
import jax
import jax.numpy as jnp

def _softmax(x, axis=-1):
    return jax.nn.softmax(x, axis=axis)

def _gelu(x):
    return jax.nn.gelu(x, approximate=True)

def _silu(x):
    return jax.nn.silu(x)

def _sigmoid(x):
    return jax.nn.sigmoid(x)

def _layernorm(x, axis=-1, eps=1e-05):
    m = jnp.mean(x, axis=axis, keepdims=True)
    v = jnp.var(x, axis=axis, keepdims=True)
    return (x - m) / jnp.sqrt(v + eps)

def _scatter_add(tgt, idx, src, axis=0):
    return tgt.at[idx].add(src)

def _segment_sum(src, seg, n):
    return jax.ops.segment_sum(src, seg, n)
kernel_name = 'mk_macaron_d2_jaxref_r8_700f4f'

def setup_inputs(seed: int=0):
    np.random.seed(seed)
    _w = jnp.asarray

    def _L0_attn_setup():
        import math
        import jax, jax.numpy as jnp
        import numpy as np
        NUM_HEADS = 16
        EMBED = 128
        B, T = (2, 256)
        key = jax.random.key(seed)
        k1, k2 = jax.random.split(key)
        x = jax.random.normal(k1, (B, T, EMBED), dtype=jnp.float32)
        bound = 1.0 / math.sqrt(NUM_HEADS * EMBED)
        weight = jax.random.uniform(k2, (NUM_HEADS * EMBED, EMBED), dtype=jnp.float32, minval=-bound, maxval=bound)
        return {'x': x, 'weight': weight}
    _L0_attn_in = _L0_attn_setup()

    def _L0_ffn_setup():
        import jax, jax.numpy as jnp
        import numpy as np
        B, S, H, I, E, K = (2, 64, 128, 64, 64, 8)
        key = jax.random.key(seed)
        ks = jax.random.split(key, 8)
        return {'hidden_states': jax.random.normal(ks[0], (B, S, H), dtype=jnp.float32), 'router_w': jax.random.normal(ks[1], (H, E), dtype=jnp.float32) * 0.02, 'shared_gate_w': jax.random.normal(ks[2], (H, I), dtype=jnp.float32) * 0.02, 'shared_up_w': jax.random.normal(ks[3], (H, I), dtype=jnp.float32) * 0.02, 'shared_down_w': jax.random.normal(ks[4], (I, H), dtype=jnp.float32) * 0.02, 'expert_gate_k': jax.random.normal(ks[5], (E, H, I), dtype=jnp.float32) * 0.02, 'expert_up_k': jax.random.normal(ks[6], (E, H, I), dtype=jnp.float32) * 0.02, 'expert_down_k': jax.random.normal(ks[7], (E, I, H), dtype=jnp.float32) * 0.02}
    _L0_ffn_in = _L0_ffn_setup()

    def _L1_attn_setup():
        import math
        import jax, jax.numpy as jnp
        import numpy as np
        B, T, D, H = (2, 1024, 128, 1)
        DH = D // H

        def _layernorm(x, g, b):
            m = x.mean(-1, keepdims=True)
            v = ((x - m) ** 2).mean(-1, keepdims=True)
            return (x - m) * jax.lax.rsqrt(v + 1e-05) * g + b

        def _l2norm(x):
            n = jnp.sqrt(jnp.sum(x * x, axis=-1, keepdims=True))
            return x / jnp.maximum(n, 1e-12)

        def _rope(x, times):
            half = x.shape[-1] // 2
            freqs = jnp.exp(-jnp.arange(half, dtype=x.dtype) * (math.log(10000.0) / half))
            th = times[:, None] * freqs[None, :]
            c = jnp.cos(th)[None, :, None, :]
            s = jnp.sin(th)[None, :, None, :]
            xr = x.reshape(x.shape[:-1] + (half, 2))
            x1, x2 = (xr[..., 0], xr[..., 1])
            out = jnp.stack([x1 * c - x2 * s, x1 * s + x2 * c], axis=-1)
            return out.reshape(x.shape)

        def _forward(x, Wq, Wk, Wv, gate_W, gate_b, p_W, p_b, clock_W, clock_b, out_W, out_b, ln1_g, ln1_b, ln2_g, ln2_b, mlp_W1, mlp_b1, mlp_W2, mlp_b2):
            Bc, Tc, Dc = x.shape
            residual = x
            xn = _layernorm(x, ln1_g, ln1_b)
            times = jnp.arange(Tc, dtype=x.dtype)
            q = _l2norm((xn @ Wq).reshape(Bc, Tc, H, DH))
            k = _l2norm((xn @ Wk).reshape(Bc, Tc, H, DH))
            v = (xn @ Wv).reshape(Bc, Tc, H, DH)
            clock = jax.nn.softplus(xn @ clock_W + clock_b).reshape(Bc, Tc, H, 1)
            q = _rope(q, times)
            k = _rope(k, times)
            gj = -jax.nn.softplus(xn @ gate_W + gate_b).reshape(Bc, Tc, H, DH)
            gj_cumprod = jnp.exp(jnp.clip(jnp.cumsum(gj, axis=1), -60.0, 50.0))
            q = q * gj_cumprod
            k = k / (gj_cumprod + 1e-08)
            p = (xn @ p_W + p_b).reshape(Bc, Tc, H, DH)
            p_max = jnp.max(p, axis=1, keepdims=True)
            p_exp = jnp.exp(p - p_max) * clock
            p_cum = jnp.cumsum(p_exp, axis=1)
            q = q / (p_cum + 1e-08)
            k = k * p_exp
            scale = 1.0 / math.sqrt(DH)
            scores = jnp.einsum('bqhd,bkhd->bhqk', q, k) * scale
            mask = jnp.tril(jnp.ones((Tc, Tc), dtype=bool))
            scores = jnp.where(mask[None, None], scores, jnp.finfo(scores.dtype).min)
            w = jax.nn.softmax(scores, axis=-1)
            out = jnp.einsum('bhqk,bkhd->bqhd', w, v).reshape(Bc, Tc, Dc)
            x2 = out @ out_W + out_b + residual
            h = _layernorm(x2, ln2_g, ln2_b)
            mlp = jax.nn.gelu(h @ mlp_W1 + mlp_b1, approximate=False) @ mlp_W2 + mlp_b2
            return x2 + mlp
        key = jax.random.key(seed)
        ks = jax.random.split(key, 11)
        s = 0.02
        f = lambda k, shp: jax.random.normal(k, shp, dtype=jnp.float32) * s
        return {'x': jax.random.normal(ks[0], (B, T, D), dtype=jnp.float32), 'Wq': f(ks[1], (D, D)), 'Wk': f(ks[2], (D, D)), 'Wv': f(ks[3], (D, D)), 'gate_W': f(ks[4], (D, D)), 'gate_b': jnp.zeros((D,), jnp.float32), 'p_W': f(ks[5], (D, D)), 'p_b': jnp.zeros((D,), jnp.float32), 'clock_W': f(ks[6], (D, H)), 'clock_b': jnp.zeros((H,), jnp.float32), 'out_W': f(ks[7], (D, D)), 'out_b': jnp.zeros((D,), jnp.float32), 'ln1_g': jnp.ones((D,), jnp.float32), 'ln1_b': jnp.zeros((D,), jnp.float32), 'ln2_g': jnp.ones((D,), jnp.float32), 'ln2_b': jnp.zeros((D,), jnp.float32), 'mlp_W1': f(ks[8], (D, 4 * D)), 'mlp_b1': jnp.zeros((4 * D,), jnp.float32), 'mlp_W2': f(ks[9], (4 * D, D)), 'mlp_b2': jnp.zeros((D,), jnp.float32)}
    _L1_attn_in = _L1_attn_setup()

    def _L1_ffn_setup():
        import jax, jax.numpy as jnp
        import numpy as np
        from jax import lax
        T, B, I, M, O = (32, 64, 128, 128, 128)

        def _xavier(key, shape):
            fan_out, fan_in = shape
            limit = float(np.sqrt(6.0 / (fan_in + fan_out)))
            return jax.random.uniform(key, shape, jnp.float32, -limit, limit)
        key = jax.random.key(seed)
        ks = jax.random.split(key, 9)
        x = jax.random.normal(ks[0], (T, B, I), jnp.float32)
        return {'x': x, 'wf': _xavier(ks[1], (M, I)), 'uf': _xavier(ks[2], (M, M)), 'bf': jnp.zeros((M,), jnp.float32), 'wi': _xavier(ks[3], (M, I)), 'ui': _xavier(ks[4], (M, M)), 'bi': jnp.zeros((M,), jnp.float32), 'wc': _xavier(ks[5], (M, I)), 'uc': _xavier(ks[6], (M, M)), 'bc': jnp.zeros((M,), jnp.float32), 'wo': _xavier(ks[7], (O, I)), 'uo': _xavier(ks[8], (O, M)), 'bo': jnp.zeros((O,), jnp.float32), 'in_c': jnp.zeros((M,), jnp.float32)}
    _L1_ffn_in = _L1_ffn_setup()
    _d = {'L0_attn_x': _L0_attn_in['x'], 'L0_attn_weight': _L0_attn_in['weight'], 'L0_ffn_router_w': _L0_ffn_in['router_w'], 'L0_ffn_shared_gate_w': _L0_ffn_in['shared_gate_w'], 'L0_ffn_shared_up_w': _L0_ffn_in['shared_up_w'], 'L0_ffn_shared_down_w': _L0_ffn_in['shared_down_w'], 'L0_ffn_expert_gate_k': _L0_ffn_in['expert_gate_k'], 'L0_ffn_expert_up_k': _L0_ffn_in['expert_up_k'], 'L0_ffn_expert_down_k': _L0_ffn_in['expert_down_k'], 'L1_attn_Wq': _L1_attn_in['Wq'], 'L1_attn_Wk': _L1_attn_in['Wk'], 'L1_attn_Wv': _L1_attn_in['Wv'], 'L1_attn_gate_W': _L1_attn_in['gate_W'], 'L1_attn_gate_b': _L1_attn_in['gate_b'], 'L1_attn_p_W': _L1_attn_in['p_W'], 'L1_attn_p_b': _L1_attn_in['p_b'], 'L1_attn_clock_W': _L1_attn_in['clock_W'], 'L1_attn_clock_b': _L1_attn_in['clock_b'], 'L1_attn_out_W': _L1_attn_in['out_W'], 'L1_attn_out_b': _L1_attn_in['out_b'], 'L1_attn_ln1_g': _L1_attn_in['ln1_g'], 'L1_attn_ln1_b': _L1_attn_in['ln1_b'], 'L1_attn_ln2_g': _L1_attn_in['ln2_g'], 'L1_attn_ln2_b': _L1_attn_in['ln2_b'], 'L1_attn_mlp_W1': _L1_attn_in['mlp_W1'], 'L1_attn_mlp_b1': _L1_attn_in['mlp_b1'], 'L1_attn_mlp_W2': _L1_attn_in['mlp_W2'], 'L1_attn_mlp_b2': _L1_attn_in['mlp_b2'], 'L1_ffn_wf': _L1_ffn_in['wf'], 'L1_ffn_uf': _L1_ffn_in['uf'], 'L1_ffn_bf': _L1_ffn_in['bf'], 'L1_ffn_wi': _L1_ffn_in['wi'], 'L1_ffn_ui': _L1_ffn_in['ui'], 'L1_ffn_bi': _L1_ffn_in['bi'], 'L1_ffn_wc': _L1_ffn_in['wc'], 'L1_ffn_uc': _L1_ffn_in['uc'], 'L1_ffn_bc': _L1_ffn_in['bc'], 'L1_ffn_wo': _L1_ffn_in['wo'], 'L1_ffn_uo': _L1_ffn_in['uo'], 'L1_ffn_bo': _L1_ffn_in['bo'], 'L1_ffn_in_c': _L1_ffn_in['in_c']}
    _x0 = _d['L0_attn_x']
    _d['L0_attn_x'] = jax.random.normal(jax.random.fold_in(jax.random.key(seed), 1), (4, 1024, 128), dtype=_x0.dtype)
    del _x0
    return _d

def reference(L0_attn_x, L0_attn_weight, L0_ffn_router_w, L0_ffn_shared_gate_w, L0_ffn_shared_up_w, L0_ffn_shared_down_w, L0_ffn_expert_gate_k, L0_ffn_expert_up_k, L0_ffn_expert_down_k, L1_attn_Wq, L1_attn_Wk, L1_attn_Wv, L1_attn_gate_W, L1_attn_gate_b, L1_attn_p_W, L1_attn_p_b, L1_attn_clock_W, L1_attn_clock_b, L1_attn_out_W, L1_attn_out_b, L1_attn_ln1_g, L1_attn_ln1_b, L1_attn_ln2_g, L1_attn_ln2_b, L1_attn_mlp_W1, L1_attn_mlp_b1, L1_attn_mlp_W2, L1_attn_mlp_b2, L1_ffn_wf, L1_ffn_uf, L1_ffn_bf, L1_ffn_wi, L1_ffn_ui, L1_ffn_bi, L1_ffn_wc, L1_ffn_uc, L1_ffn_bc, L1_ffn_wo, L1_ffn_uo, L1_ffn_bo, L1_ffn_in_c):

    def _L0_attn_ref(x, weight):
        import math
        import jax, jax.numpy as jnp
        import numpy as np
        NUM_HEADS = 16
        EMBED = 128
        B, T = (2, 256)
        b, t, c = x.shape
        nh = NUM_HEADS
        hs = c // nh
        y = x.reshape(b, t, nh, hs).transpose(0, 2, 1, 3)
        scores = jnp.einsum('bhtk,bhsk->bhts', y, y) / math.sqrt(hs)
        attn = jax.nn.softmax(scores, axis=-1)
        o = jnp.einsum('bhts,bsc->bhtc', attn, x)
        o = o.transpose(0, 2, 1, 3).reshape(b, t, nh * c)
        return o @ weight

    def _L0_ffn_ref(hidden_states, router_w, shared_gate_w, shared_up_w, shared_down_w, expert_gate_k, expert_up_k, expert_down_k):
        import jax, jax.numpy as jnp
        import numpy as np
        B, S, H, I, E, K = (2, 64, 128, 64, 64, 8)
        logits = jnp.einsum('bsh,he->bse', hidden_states.astype(jnp.float32), router_w)
        affinity = jax.nn.sigmoid(logits)
        top_scores, top_idx = jax.lax.top_k(affinity, K)
        top_w = top_scores / (jnp.sum(top_scores, axis=-1, keepdims=True) + 1e-09)
        one_hot = jax.nn.one_hot(top_idx, E, dtype=top_w.dtype)
        router_mask = jnp.einsum('bske,bsk->bse', one_hot, top_w).astype(hidden_states.dtype)
        shared = jnp.einsum('bsi,ih->bsh', jax.nn.silu(hidden_states @ shared_gate_w) * (hidden_states @ shared_up_w), shared_down_w)
        gate_out = jnp.einsum('bsh,ehi->bsei', hidden_states, expert_gate_k)
        up_out = jnp.einsum('bsh,ehi->bsei', hidden_states, expert_up_k)
        expert_act = jax.nn.silu(gate_out) * up_out
        routed = jnp.einsum('bsei,eih->bsh', expert_act * router_mask[..., None], expert_down_k)
        return shared + routed

    def _L1_attn_ref(x, Wq, Wk, Wv, gate_W, gate_b, p_W, p_b, clock_W, clock_b, out_W, out_b, ln1_g, ln1_b, ln2_g, ln2_b, mlp_W1, mlp_b1, mlp_W2, mlp_b2):
        import math
        import jax, jax.numpy as jnp
        import numpy as np
        B, T, D, H = (2, 1024, 128, 1)
        DH = D // H

        def _layernorm(x, g, b):
            m = x.mean(-1, keepdims=True)
            v = ((x - m) ** 2).mean(-1, keepdims=True)
            return (x - m) * jax.lax.rsqrt(v + 1e-05) * g + b

        def _l2norm(x):
            n = jnp.sqrt(jnp.sum(x * x, axis=-1, keepdims=True))
            return x / jnp.maximum(n, 1e-12)

        def _rope(x, times):
            half = x.shape[-1] // 2
            freqs = jnp.exp(-jnp.arange(half, dtype=x.dtype) * (math.log(10000.0) / half))
            th = times[:, None] * freqs[None, :]
            c = jnp.cos(th)[None, :, None, :]
            s = jnp.sin(th)[None, :, None, :]
            xr = x.reshape(x.shape[:-1] + (half, 2))
            x1, x2 = (xr[..., 0], xr[..., 1])
            out = jnp.stack([x1 * c - x2 * s, x1 * s + x2 * c], axis=-1)
            return out.reshape(x.shape)

        def _forward(x, Wq, Wk, Wv, gate_W, gate_b, p_W, p_b, clock_W, clock_b, out_W, out_b, ln1_g, ln1_b, ln2_g, ln2_b, mlp_W1, mlp_b1, mlp_W2, mlp_b2):
            Bc, Tc, Dc = x.shape
            residual = x
            xn = _layernorm(x, ln1_g, ln1_b)
            times = jnp.arange(Tc, dtype=x.dtype)
            q = _l2norm((xn @ Wq).reshape(Bc, Tc, H, DH))
            k = _l2norm((xn @ Wk).reshape(Bc, Tc, H, DH))
            v = (xn @ Wv).reshape(Bc, Tc, H, DH)
            clock = jax.nn.softplus(xn @ clock_W + clock_b).reshape(Bc, Tc, H, 1)
            q = _rope(q, times)
            k = _rope(k, times)
            gj = -jax.nn.softplus(xn @ gate_W + gate_b).reshape(Bc, Tc, H, DH)
            gj_cumprod = jnp.exp(jnp.clip(jnp.cumsum(gj, axis=1), -60.0, 50.0))
            q = q * gj_cumprod
            k = k / (gj_cumprod + 1e-08)
            p = (xn @ p_W + p_b).reshape(Bc, Tc, H, DH)
            p_max = jnp.max(p, axis=1, keepdims=True)
            p_exp = jnp.exp(p - p_max) * clock
            p_cum = jnp.cumsum(p_exp, axis=1)
            q = q / (p_cum + 1e-08)
            k = k * p_exp
            scale = 1.0 / math.sqrt(DH)
            scores = jnp.einsum('bqhd,bkhd->bhqk', q, k) * scale
            mask = jnp.tril(jnp.ones((Tc, Tc), dtype=bool))
            scores = jnp.where(mask[None, None], scores, jnp.finfo(scores.dtype).min)
            w = jax.nn.softmax(scores, axis=-1)
            out = jnp.einsum('bhqk,bkhd->bqhd', w, v).reshape(Bc, Tc, Dc)
            x2 = out @ out_W + out_b + residual
            h = _layernorm(x2, ln2_g, ln2_b)
            mlp = jax.nn.gelu(h @ mlp_W1 + mlp_b1, approximate=False) @ mlp_W2 + mlp_b2
            return x2 + mlp
        return _forward(x, Wq, Wk, Wv, gate_W, gate_b, p_W, p_b, clock_W, clock_b, out_W, out_b, ln1_g, ln1_b, ln2_g, ln2_b, mlp_W1, mlp_b1, mlp_W2, mlp_b2)

    def _L1_ffn_ref(x, wf, uf, bf, wi, ui, bi, wc, uc, bc, wo, uo, bo, in_c):
        import jax, jax.numpy as jnp
        import numpy as np
        from jax import lax
        T, B, I, M, O = (32, 64, 128, 128, 128)

        def _xavier(key, shape):
            fan_out, fan_in = shape
            limit = float(np.sqrt(6.0 / (fan_in + fan_out)))
            return jax.random.uniform(key, shape, jnp.float32, -limit, limit)
        batch = x.shape[1]
        c0 = jnp.broadcast_to(in_c, (batch, in_c.shape[0]))

        def step(c, xt):
            ft = jax.nn.sigmoid(xt @ wf.T + c @ uf.T + bf)
            it = jax.nn.sigmoid(xt @ wi.T + c @ ui.T + bi)
            gt = jnp.tanh(xt @ wc.T + c @ uc.T + bc)
            c = ft * c + it * gt
            return (c, None)
        c_final, _ = lax.scan(step, c0, x)
        h = jnp.tanh(jnp.einsum('tbi,oi->tbo', x, wo) + c_final @ uo.T + bo)
        return h
    x = L0_attn_x
    x = x + 0.5 * _L0_ffn_ref(_layernorm(x, axis=-1), L0_ffn_router_w, L0_ffn_shared_gate_w, L0_ffn_shared_up_w, L0_ffn_shared_down_w, L0_ffn_expert_gate_k, L0_ffn_expert_up_k, L0_ffn_expert_down_k)
    x = x + _L0_attn_ref(_layernorm(x, axis=-1), L0_attn_weight)
    x = x + 0.5 * _L0_ffn_ref(_layernorm(x, axis=-1), L0_ffn_router_w, L0_ffn_shared_gate_w, L0_ffn_shared_up_w, L0_ffn_shared_down_w, L0_ffn_expert_gate_k, L0_ffn_expert_up_k, L0_ffn_expert_down_k)
    x = x + 0.5 * _L1_ffn_ref(_layernorm(x, axis=-1), L1_ffn_wf, L1_ffn_uf, L1_ffn_bf, L1_ffn_wi, L1_ffn_ui, L1_ffn_bi, L1_ffn_wc, L1_ffn_uc, L1_ffn_bc, L1_ffn_wo, L1_ffn_uo, L1_ffn_bo, L1_ffn_in_c)
    x = x + _L1_attn_ref(_layernorm(x, axis=-1), L1_attn_Wq, L1_attn_Wk, L1_attn_Wv, L1_attn_gate_W, L1_attn_gate_b, L1_attn_p_W, L1_attn_p_b, L1_attn_clock_W, L1_attn_clock_b, L1_attn_out_W, L1_attn_out_b, L1_attn_ln1_g, L1_attn_ln1_b, L1_attn_ln2_g, L1_attn_ln2_b, L1_attn_mlp_W1, L1_attn_mlp_b1, L1_attn_mlp_W2, L1_attn_mlp_b2)
    x = x + 0.5 * _L1_ffn_ref(_layernorm(x, axis=-1), L1_ffn_wf, L1_ffn_uf, L1_ffn_bf, L1_ffn_wi, L1_ffn_ui, L1_ffn_bi, L1_ffn_wc, L1_ffn_uc, L1_ffn_bc, L1_ffn_wo, L1_ffn_uo, L1_ffn_bo, L1_ffn_in_c)
    return x

_drawn_inputs = setup_inputs


def setup_inputs(seed=0):
    import zlib

    import numpy as np

    out = dict(_drawn_inputs(seed))
    spreads = {'L1_attn_gate_b': (0.0, 2.0),
     'L1_attn_p_b': (0.0, 0.1),
     'L1_attn_out_b': (0.0, 0.374),
     'L1_attn_ln1_g': (1.0, 0.6),
     'L1_attn_ln1_b': (0.0, 0.8),
     'L1_attn_ln2_g': (1.0, 0.6),
     'L1_attn_ln2_b': (0.0, 2.0),
     'L1_attn_mlp_b1': (0.0, 0.79),
     'L1_attn_mlp_b2': (0.0, 0.367),
     'L1_ffn_bf': (0.0, 2.0),
     'L1_ffn_bi': (0.0, 2.0),
     'L1_ffn_bc': (0.0, 0.574),
     'L1_ffn_bo': (0.0, 0.422),
     'L1_ffn_in_c': (0.0, 0.619)}
    factors = {'L0_ffn_router_w': 8.0,
     'L0_ffn_shared_gate_w': 8.0,
     'L0_ffn_shared_up_w': 8.0,
     'L0_ffn_shared_down_w': 8.0,
     'L0_ffn_expert_gate_k': 8.0,
     'L0_ffn_expert_up_k': 8.0,
     'L0_ffn_expert_down_k': 8.0,
     'L1_attn_Wq': 64.0,
     'L1_attn_Wk': 64.0,
     'L1_attn_Wv': 8.0,
     'L1_attn_gate_W': 64.0,
     'L1_attn_p_W': 64.0,
     'L1_attn_clock_W': 64.0,
     'L1_attn_out_W': 8.0,
     'L1_ffn_uf': 3.405,
     'L1_ffn_ui': 3.523}
    for name, (base, spread) in spreads.items():
        noise = np.random.default_rng([zlib.crc32(name.encode()), seed]).standard_normal(out[name].shape)
        drawn = base * np.exp(spread * noise) if base else spread * noise
        out[name] = jnp.asarray(drawn.astype(out[name].dtype))
    for name, factor in factors.items():
        out[name] = (out[name] * factor).astype(out[name].dtype)
    return out
```

```python
import math
from contextlib import ExitStack

import concourse.bass as bass
from concourse import mybir
from concourse.alu_op_type import AluOpType as ALU

F32 = mybir.dt.float32
F32R = mybir.dt.float32r
ACT = mybir.ActivationFunctionType
ds = bass.ds

P = 128
BATCH, T = 4, 1024
TOKENS = BATCH * T
BANK = 512
CHUNKS = TOKENS // BANK
HALVES = T // BANK
EPS = 1e-5

EXPERTS, HIDDEN, TOP = 64, 64, 8
PAIRS = EXPERTS * HIDDEN // P
GROUP = 4
GROUPS = PAIRS // GROUP
LAG = 3

HEADS, HEAD = 16, 8
QUAD = 4
TILES = T // P


def sb_in(ctx, nc):
    def sb(name, shape, dt=F32):
        return ctx.enter_context(nc.sbuf_tensor(name, shape, dt))
    return sb


def sems_in(ctx, nc, tag):
    handles = []

    def sem(name):
        handles.append(nc.alloc_semaphore(name=f"{tag}_{name}"))
        return handles[-1]

    def clear():
        nc.clear_and_free_semaphores(handles)
        nc.all_engine_barrier()

    ctx.callback(clear)
    return sem


def after(eng, sem, count):
    if isinstance(count, int) and count <= 0:
        return
    eng.wait_ge(sem, count)


def wait_apart(eng, sem, count, passed):
    eng.wait_ge(sem, count)
    eng.sem_inc(passed, 1)


def f(ap):
    return ap.bitcast(F32)


def product(pe, out, w, x, first=True, last=True):
    (w_hi, w_lo), (x_hi, x_lo) = w, x
    pe.matmul(out, w_lo, x_hi, start=first, stop=False, skip_group_check=True)
    pe.matmul(out, w_hi, x_lo, start=False, stop=False, skip_group_check=True)
    return pe.matmul(out, w_hi, x_hi, start=False, stop=last, skip_group_check=True)


def load_constants(nc, loads, exact):
    with ExitStack() as ctx:
        sem = sems_in(ctx, nc, "constants")
        loaded, exact_loaded, exact_ready = (sem(name) for name in
                                             ("constants_loaded", "exact_loaded", "exact_ready"))
        raws = [sb_in(ctx, nc)(f"exact_raw{i}", tile.shape) for i, (_, tile) in enumerate(exact)]
        with nc.Block() as block:
            @block.sync
            def _(sp):
                for tile, source in loads:
                    sp.dma_start(tile, source).then_inc(loaded, 16)
                sp.wait_ge(loaded, 16 * len(loads))

            @block.scalar
            def _(act):
                for raw, (source, _) in zip(raws, exact):
                    act.dma_start(raw[:, :], source).then_inc(exact_loaded, 16)

            @block.vector
            def _(dve):
                dve.wait_ge(exact_loaded, 16 * len(exact))
                for raw, (_, tile) in zip(raws, exact):
                    dve.tensor_copy(tile, raw[:, :]).then_inc(exact_ready, 1)
                dve.wait_ge(exact_ready, len(exact))


def load_split(nc, tag, weights):
    with ExitStack() as ctx:
        sb, sem = sb_in(ctx, nc), sems_in(ctx, nc, tag)
        raws = [sb(f"{tag}_raw{i}", [P, hi.shape[1]]) for i, (_, hi, _) in enumerate(weights)]
        high = sem("high")
        low = sem("low")
        loaded = [sem(f"loaded{i}") for i in range(len(weights))]
        with nc.Block() as block:
            @block.sync
            def _(sp):
                for raw, (source, _, _), s in zip(raws, weights, loaded):
                    sp.dma_start(raw[:, :], source).then_inc(s, 16)

            @block.scalar
            def _(act):
                for raw, (_, hi, _), s in zip(raws, weights, loaded):
                    act.wait_ge(s, 16)
                    act.copy(hi, raw[:, :]).then_inc(high, 1)

            @block.vector
            def _(dve):
                for n, (raw, (_, hi, lo)) in enumerate(zip(raws, weights)):
                    dve.wait_ge(high, n + 1)
                    dve.tensor_tensor(lo, raw[:, :], f(hi), ALU.subtract).then_inc(low, 1)
                dve.wait_ge(low, len(weights))


def layernorm(nc, tag, psum, consts, x, n_hi, n_lo, affine=None, keep=None):
    inv, eps, identity, row_spread = consts["inv"], consts["eps"], consts["identity"], consts["row_spread"]
    SET = 4
    COLUMNS = SET * BANK // P
    MEAN, SCALE = 0, 4
    with ExitStack() as ctx:
        sb, sem = sb_in(ctx, nc), sems_in(ctx, nc, tag)
        centered = sb(f"{tag}_centered", [P, SET, BANK])
        squares = sb(f"{tag}_squares", [P, SET, BANK])
        deviation = sb(f"{tag}_deviation", [P, COLUMNS])
        inverse = sb(f"{tag}_inverse", [P, 2, 32])
        inverse_rows = sb(f"{tag}_inverse_rows", [2 * 32, P], F32R)
        normal = sb(f"{tag}_normal", [P, SET, BANK])
        clear = sem("clear")
        mean_ready, centered_ready, squares_ready = sem("mean"), sem("centered"), sem("squares")
        variance_ready, deviation_ready, inverse_ready, turned = sem("variance"), sem("deviation"), sem("inverse"), sem("turned")
        rows_high, rows_ready, scale_ready, scaled_ready = sem("rows_high"), sem("rows"), sem("scale"), sem("scaled")
        normal_ready = scaled_ready if affine is None else sem("normal")
        high_ready, low_ready = sem("high"), sem("low")
        pe_passed = sem("pe_passed")

        with nc.Block() as block:
            @block.tensor
            def _(pe):
                with pe.Fori(0, CHUNKS // SET) as r:
                    for j in range(SET):
                        pe.matmul(psum[:, MEAN + j, :], inv, x[:, ds(r * (SET * BANK) + j * BANK, BANK)],
                                  start=True, stop=True).then_inc(mean_ready, 1)
                    for j in range(SET):
                        pe.wait_ge(squares_ready, r * SET + (j + 1))
                        for q in range(BANK // P):
                            column = j * (BANK // P) + q
                            last = pe.matmul(psum[:, SCALE, column:column + 1], squares[:, j, q * P:(q + 1) * P],
                                             inv[:, 0:1], start=column == 0, stop=column == COLUMNS - 1,
                                             skip_group_check=True)
                    last.then_inc(variance_ready, 1)
                    wait_apart(pe, inverse_ready, r + 1, pe_passed)
                    pe.transpose(psum[0:64, SCALE + 1, 0:P], inverse[:, :, :].rearrange("p a b -> p (a b)"),
                                 identity).then_inc(turned, 1)
                    pe.wait_ge(rows_ready, r + 1)
                    for j in range(SET):
                        for q in range(BANK // P):
                            column = j * (BANK // P) + q
                            last = pe.matmul(psum[:, SCALE + j, q * P:(q + 1) * P],
                                             row_spread[:, column * P:(column + 1) * P], inverse_rows[:, :],
                                             start=q == 0, stop=q == BANK // P - 1, skip_group_check=True)
                        last.then_inc(scale_ready, 1)
                    pe.wait_ge(scaled_ready, r * SET + SET)

            @block.scalar
            def _(act):
                with act.Fori(0, CHUNKS // SET) as r:
                    for j in range(SET):
                        act.wait_ge(centered_ready, r * SET + (j + 1))
                        act.activation(squares[:, j, :], centered[:, j, :], ACT.Square).then_inc(squares_ready, 1)
                    act.wait_ge(variance_ready, r + 1)
                    act.activation(deviation[:, :], psum[:, SCALE, 0:COLUMNS], ACT.Sqrt, bias=eps).then_inc(deviation_ready, 1)
                    if keep is None:
                        for j in range(SET):
                            act.wait_ge(normal_ready, r * SET + (j + 1))
                            act.copy(n_hi[:, ds(r * (SET * BANK) + j * BANK, BANK)], normal[:, j, :]).then_inc(high_ready, 1)

            @block.vector
            def _(dve):
                dve.memset(inverse[:, :, :], 0.0).then_inc(clear, 1)
                dve.wait_ge(clear, 1)
                with dve.Fori(0, CHUNKS // SET) as r:
                    for j in range(SET):
                        at = ds(r * (SET * BANK) + j * BANK, BANK)
                        dve.wait_ge(mean_ready, r * SET + (j + 1))
                        dve.tensor_tensor(centered[:, j, :], x[:, at], psum[:, MEAN + j, :],
                                          ALU.subtract).then_inc(centered_ready, 1)
                    dve.wait_ge(deviation_ready, r + 1)
                    dve.reciprocal(inverse[:, :, 0:COLUMNS],
                                   deviation[:, :].unsqueeze(1).to_broadcast([P, 2, COLUMNS])).then_inc(inverse_ready, 1)
                    dve.wait_ge(turned, r + 1)
                    dve.tensor_copy(inverse_rows[:, :], psum[0:64, SCALE + 1, 0:P]).then_inc(rows_high, 1)
                    dve.wait_ge(rows_high, r + 1)
                    dve.tensor_tensor(inverse_rows[32:64, :], psum[32:64, SCALE + 1, 0:P], f(inverse_rows[32:64, :]),
                                      ALU.subtract).then_inc(rows_ready, 1)
                    for j in range(SET):
                        at = ds(r * (SET * BANK) + j * BANK, BANK)
                        to = normal[:, j, :] if keep is None else keep[:, at]
                        dve.wait_ge(scale_ready, r * SET + (j + 1))
                        scaled = dve.tensor_tensor(to, centered[:, j, :], psum[:, SCALE + j, :], ALU.mult)
                        scaled.then_inc(scaled_ready, 1)
                        if affine is not None:
                            dve.wait_ge(scaled_ready, r * SET + (j + 1))
                            dve.tensor_scalar(to, to, affine[0], affine[1], ALU.mult, ALU.add).then_inc(normal_ready, 1)
                    if keep is None:
                        dve.wait_ge(low_ready, r * SET + SET)

            @block.gpsimd
            def _(pool):
                if keep is None:
                    with pool.Fori(0, CHUNKS // SET) as r:
                        for j in range(SET):
                            at = ds(r * (SET * BANK) + j * BANK, BANK)
                            pool.wait_ge(high_ready, r * SET + (j + 1))
                            pool.tensor_tensor(n_lo[:, at], normal[:, j, :], f(n_hi[:, at]),
                                               ALU.subtract).then_inc(low_ready, 1)


def route(nc, tag, psum, consts, router, n_hi, n_lo, mask):
    identity = consts["identity"]
    with ExitStack() as ctx:
        sb, sem = sb_in(ctx, nc), sems_in(ctx, nc, tag)
        affinity = sb(f"{tag}_affinity", [P, 2, BANK])
        best = sb(f"{tag}_best", [P, 2, 4, TOP])
        rest = sb(f"{tag}_rest", [P, 2, 4, EXPERTS])
        chosen = sb(f"{tag}_chosen", [P, 2, 4, EXPERTS])
        total = sb(f"{tag}_total", [P, 2, 4])
        weights = sb(f"{tag}_weights", [P, 2, 4, 2, EXPERTS])
        logits_ready, affinity_ready, turned, best_found = sem("logits"), sem("affinity"), sem("turned"), sem("best")
        rest_ready, chosen_ready, total_ready, inverse_ready = sem("rest"), sem("chosen"), sem("total"), sem("inverse")
        weights_ready, weights_turned, high_ready, mask_ready = sem("weights"), sem("weights_turned"), sem("high"), sem("mask")
        passed = sem("passed")
        LOGITS, TURNED, MASK = 0, 2, 4

        with nc.Block() as block:
            @block.tensor
            def _(pe):
                with pe.Fori(0, CHUNKS // 2) as r:
                    for j in range(2):
                        at = ds(r * (2 * BANK) + j * BANK, BANK)
                        product(pe, psum[:, LOGITS + j, :], router, (n_hi[:, at], n_lo[:, at])).then_inc(logits_ready, 1)
                    for j in range(2):
                        pe.wait_ge(affinity_ready, r * 2 + (j + 1))
                        for q in range(4):
                            turn = pe.transpose(psum[:, TURNED + j, q * P:(q + 1) * P],
                                                affinity[:, j, q * P:(q + 1) * P], identity)
                        turn.then_inc(turned, 1)
                    for j in range(2):
                        pe.wait_ge(weights_ready, r * 8 + (j + 1) * 4)
                        for q in range(4):
                            turn = pe.transpose(psum[:, MASK + j, q * P:(q + 1) * P],
                                                weights[:, j, q, :, :].rearrange("p a e -> p (a e)"), identity)
                        turn.then_inc(weights_turned, 1)
                    pe.wait_ge(mask_ready, r * 2 + 2)

            @block.scalar
            def _(act):
                with act.Fori(0, CHUNKS // 2) as r:
                    for j in range(2):
                        act.wait_ge(logits_ready, r * 2 + (j + 1))
                        act.activation(affinity[:, j, :], psum[:, LOGITS + j, :], ACT.Sigmoid).then_inc(affinity_ready, 1)
                    act.wait_ge(turned, r * 2 + 2)

            @block.vector
            def _(dve):
                with dve.Fori(0, CHUNKS // 2) as r:
                    for j in range(2):
                        def scores(q):
                            return psum[:, TURNED + j, q * P:q * P + EXPERTS]

                        wait_apart(dve, turned, r * 2 + (j + 1), passed)
                        for q in range(4):
                            dve.max(best[:, j, q, :], scores(q)).then_inc(best_found, 1)
                        for q in range(4):
                            wait_apart(dve, best_found, r * 8 + (j * 4 + q + 1), passed)
                            dve.match_replace(out=rest[:, j, q, :], in_to_replace=best[:, j, q, :],
                                              in_values=scores(q), imm_value=-1.0).then_inc(rest_ready, 1)
                        for q in range(4):
                            dve.wait_ge(rest_ready, r * 8 + (j * 4 + q + 1))
                            dve.scalar_tensor_tensor(out=chosen[:, j, q, :], in0=rest[:, j, q, :], scalar=0.0,
                                                     in1=scores(q), op0=ALU.is_lt, op1=ALU.mult,
                                                     accum_out=total[:, j, q:q + 1]).then_inc(chosen_ready, 1)
                        dve.wait_ge(chosen_ready, r * 8 + (j * 4 + 4))
                        dve.tensor_scalar(total[:, j, :], total[:, j, :], 1e-9, 2.0, ALU.add,
                                          ALU.mult).then_inc(total_ready, 1)
                        dve.wait_ge(total_ready, r * 2 + (j + 1))
                        dve.reciprocal(total[:, j, :], total[:, j, :]).then_inc(inverse_ready, 1)
                        dve.wait_ge(inverse_ready, r * 2 + (j + 1))
                        for q in range(4):
                            dve.tensor_scalar(weights[:, j, q, :, :],
                                              chosen[:, j, q, :].unsqueeze(1).to_broadcast([P, 2, EXPERTS]),
                                              total[:, j, q:q + 1], None, ALU.mult).then_inc(weights_ready, 1)
                    for j in range(2):
                        at = ds(r * (2 * BANK) + j * BANK, BANK)
                        dve.wait_ge(weights_turned, r * 2 + (j + 1))
                        dve.tensor_copy(mask[:, at], psum[:, MASK + j, :]).then_inc(high_ready, 1)
                        dve.wait_ge(high_ready, r * 2 + (j + 1))
                        dve.tensor_tensor(mask[EXPERTS:P, at], psum[EXPERTS:P, MASK + j, :],
                                          f(mask[EXPERTS:P, at]), ALU.subtract).then_inc(mask_ready, 1)
                    dve.wait_ge(mask_ready, r * 2 + 2)


def shared_expert(nc, tag, psum, weights, n_hi, n_lo, x):
    gate, up, down = weights
    with ExitStack() as ctx:
        sb, sem = sb_in(ctx, nc), sems_in(ctx, nc, tag)
        silu = sb(f"{tag}_silu", [P, 2, BANK])
        hidden = sb(f"{tag}_hidden", [P, 2, BANK])
        hi = sb(f"{tag}_hi", [P, 2, BANK], F32R)
        lo = sb(f"{tag}_lo", [P, 2, BANK], F32R)
        up_ready, silu_ready, hidden_ready = sem("up"), sem("silu"), sem("hidden")
        high_ready, low_ready, down_ready, added = sem("high"), sem("low"), sem("down"), sem("added")
        GATE, UP, DOWN = 0, 2, 4
        with nc.Block() as block:
            @block.tensor
            def _(pe):
                with pe.Fori(0, CHUNKS // 2) as r:
                    for j in range(2):
                        at = ds(r * (2 * BANK) + j * BANK, BANK)
                        product(pe, psum[:, GATE + j, :], gate, (n_hi[:, at], n_lo[:, at]))
                        product(pe, psum[:, UP + j, :], up, (n_hi[:, at], n_lo[:, at])).then_inc(up_ready, 1)
                    for j in range(2):
                        pe.wait_ge(low_ready, r * 2 + (j + 1))
                        product(pe, psum[:, DOWN + j, :], down, (hi[:, j, :], lo[:, j, :])).then_inc(down_ready, 1)
                    pe.wait_ge(added, r * 2 + 2)

            @block.scalar
            def _(act):
                with act.Fori(0, CHUNKS // 2) as r:
                    for j in range(2):
                        act.wait_ge(up_ready, r * 2 + (j + 1))
                        act.activation(silu[:, j, :], psum[:, GATE + j, :], ACT.Silu).then_inc(silu_ready, 1)
                    for j in range(2):
                        act.wait_ge(hidden_ready, r * 2 + (j + 1))
                        act.copy(hi[:, j, :], hidden[:, j, :]).then_inc(high_ready, 1)
                    act.wait_ge(down_ready, r * 2 + 2)

            @block.vector
            def _(dve):
                with dve.Fori(0, CHUNKS // 2) as r:
                    for j in range(2):
                        dve.wait_ge(silu_ready, r * 2 + (j + 1))
                        dve.scalar_tensor_tensor(out=hidden[:, j, :], in0=silu[:, j, :], scalar=0.25,
                                                 in1=psum[:, UP + j, :], op0=ALU.mult,
                                                 op1=ALU.mult).then_inc(hidden_ready, 1)
                    for j in range(2):
                        dve.wait_ge(high_ready, r * 2 + (j + 1))
                        dve.tensor_tensor(lo[:, j, :], hidden[:, j, :], f(hi[:, j, :]), ALU.subtract).then_inc(low_ready, 1)
                    for j in range(2):
                        at = ds(r * (2 * BANK) + j * BANK, BANK)
                        dve.wait_ge(down_ready, r * 2 + (j + 1))
                        dve.tensor_tensor(x[:, at], x[:, at], psum[:, DOWN + j, :], ALU.add).then_inc(added, 1)
                    dve.wait_ge(added, r * 2 + 2)


def experts(nc, tag, psum, dram, n_hi, n_lo, mask, x):
    gate_dram, up_dram, down_dram, pick_dram = dram
    COLS = GROUP * P
    PER = CHUNKS * GROUP
    PARTS = 3
    GATE, UP, SPREAD, DOWN = 0, 2, 4, 6
    with ExitStack() as ctx:
        sb, sem = sb_in(ctx, nc), sems_in(ctx, nc, tag)
        pick_all = sb(f"{tag}_pick_all", [P, PAIRS * P], F32R)
        with ExitStack() as first:
            pick_raw = sb_in(first, nc)(f"{tag}_pick_raw", [P, PAIRS * P])
            pick_loaded, pick_ready = sem("pick_loaded"), sem("pick_ready")
            with nc.Block() as block:
                @block.sync
                def _(sp):
                    sp.dma_start(pick_raw[:, :], pick_dram).then_inc(pick_loaded, 16)

                @block.vector
                def _(dve):
                    dve.wait_ge(pick_loaded, 16)
                    dve.tensor_copy(pick_all[:, :], pick_raw[:, :]).then_inc(pick_ready, 1)
                    dve.wait_ge(pick_ready, 1)
        raw = sb(f"{tag}_raw", [P, 2, PARTS, COLS])
        w_hi = sb(f"{tag}_w_hi", [P, 2, PARTS, COLS], F32R)
        w_lo = sb(f"{tag}_w_lo", [P, 2, PARTS, COLS], F32R)
        pick = sb(f"{tag}_pick", [P, 2, COLS], F32R)
        silu = sb(f"{tag}_silu", [P, 2, BANK])
        gated = sb(f"{tag}_gated", [P, 2, BANK])
        hidden = sb(f"{tag}_hidden", [P, 2, BANK])
        hi = sb(f"{tag}_hi", [P, GROUP, BANK], F32R)
        lo = sb(f"{tag}_lo", [P, GROUP, BANK], F32R)
        loaded = [sem("loaded_even"), sem("loaded_odd")]
        picked, high_split, low_split = [sem("picked_even"), sem("picked_odd")], sem("high_split"), sem("low_split")
        up_ready, mask_spread, silu_ready, gated_ready = sem("up"), sem("mask_spread"), sem("silu"), sem("gated")
        hidden_ready, high_ready, low_ready = sem("hidden"), sem("high"), sem("low")
        down_done, added, passed = sem("down"), sem("added"), sem("passed")

        def walk(eng, body):
            def two_groups(k):
                for parity in range(2):
                    body(k, parity, 0)
                    with eng.Fori(1, CHUNKS // 2) as pair:
                        body(k, parity, pair)
            two_groups(0)
            with eng.Fori(1, GROUPS // 2) as k:
                two_groups(k)

        def unit(k, parity, pair, j, p):
            return k * (2 * PER) + pair * (2 * GROUP) + (parity * PER + j * GROUP + p)

        def next_group_loads(k, parity):
            return k * (16 * PARTS) + 16 * PARTS * (1 + parity)

        with nc.Block() as block:
            @block.sync
            def _(sp):
                def load(k, parity, source_group):
                    splits = k * (2 * PARTS) + PARTS * (parity - 1)
                    if isinstance(splits, int):
                        after(sp, low_split, splits)
                    else:
                        wait_apart(sp, low_split, splits, passed)
                    for m, source in enumerate((gate_dram, up_dram, down_dram)):
                        sp.dma_start(raw[:, parity, m, :],
                                     source[:, ds(source_group * COLS, COLS)]).then_inc(loaded[parity], 16)

                def load_pick(k, parity):
                    spreads = k * (2 * PER) + PER * (parity - 1)
                    if isinstance(spreads, int):
                        after(sp, mask_spread, spreads)
                    else:
                        wait_apart(sp, mask_spread, spreads, passed)
                    sp.dma_start(f(pick[:, parity, :]),
                                 f(pick_all[:, ds((k * 2 + parity) * COLS, COLS)])).then_inc(picked[parity], 16)

                for parity in range(2):
                    load(0, parity, parity)
                    load_pick(0, parity)
                with sp.Fori(1, GROUPS // 2) as k:
                    for parity in range(2):
                        load(k, parity, k * 2 + parity)
                        load_pick(k, parity)
                load(GROUPS // 2, 0, 0)

            @block.tensor
            def _(pe):
                def down(k, parity, pair, j, p):
                    m, pm = unit(k, parity, pair, j, p) - LAG, (p - LAG) % GROUP
                    chunk_before = p < LAG
                    group_before = chunk_before and j == 0 and isinstance(pair, int)
                    w_at = 1 - parity if group_before else parity
                    bank = DOWN + ((j + 1) % 2 if chunk_before else j)
                    if isinstance(m, int) and m < 0:
                        return
                    pe.wait_ge(low_ready, m + 1)
                    if pm == 0:
                        count = (k * (2 * CHUNKS) + pair * 2) + (parity * CHUNKS + j - chunk_before - 1)
                        after(pe, added, count)
                    cols = slice(pm * P, (pm + 1) * P)
                    product(pe, psum[:, bank, :], (w_hi[:, w_at, 2, cols], w_lo[:, w_at, 2, cols]),
                            (hi[:, pm, :], lo[:, pm, :]), first=pm == 0, last=pm == GROUP - 1).then_inc(down_done, 1)

                def body(k, parity, pair):
                    if isinstance(pair, int):
                        pe.wait_ge(low_split, k * (2 * PARTS) + PARTS * (parity + 1))
                        pe.wait_ge(picked[parity], k * 16 + 16)
                    for j in range(2):
                        tokens = ds(pair * (2 * BANK) + j * BANK, BANK)
                        n_pair = (n_hi[:, tokens], n_lo[:, tokens])
                        for p in range(GROUP):
                            n = unit(k, parity, pair, j, p)
                            cols = slice(p * P, (p + 1) * P)
                            after(pe, gated_ready, n - 1)
                            product(pe, psum[:, GATE + p % 2, :], (w_hi[:, parity, 0, cols], w_lo[:, parity, 0, cols]), n_pair)
                            product(pe, psum[:, UP + p % 2, :], (w_hi[:, parity, 1, cols], w_lo[:, parity, 1, cols]),
                                    n_pair).then_inc(up_ready, 1)
                            after(pe, hidden_ready, n - 1)
                            pe.matmul(psum[:, SPREAD + p % 2, :], pick[:, parity, cols], mask[:, tokens],
                                      start=True, stop=True).then_inc(mask_spread, 1)
                            down(k, parity, pair, j, p)

                walk(pe, body)
                for p in range(LAG):
                    down(GROUPS // 2, 0, 0, 0, p)

            @block.scalar
            def _(act):
                def high(n, p):
                    act.wait_ge(hidden_ready, n + 1)
                    after(act, down_done, n - (GROUP - 1))
                    act.copy(hi[:, p, :], hidden[:, p % 2, :]).then_inc(high_ready, 1)

                def body(k, parity, pair):
                    for j in range(2):
                        for p in range(GROUP):
                            n = unit(k, parity, pair, j, p)
                            act.wait_ge(up_ready, n + 1)
                            after(act, gated_ready, n - 1)
                            act.activation(silu[:, p % 2, :], psum[:, GATE + p % 2, :], ACT.Silu).then_inc(silu_ready, 1)
                            if not isinstance(n, int) or n > 0:
                                high(n - 1, (p - 1) % GROUP)

                walk(act, body)
                high(GROUPS * PER - 1, GROUP - 1)

            @block.vector
            def _(dve):
                def add(k, parity, pair, j):
                    chunks = (k * (2 * CHUNKS) + pair * 2) + (parity * CHUNKS + j)
                    if isinstance(chunks, int) and chunks <= 0:
                        return
                    tokens = ds(pair * (2 * BANK) + (j - 1) * BANK, BANK)
                    if j == 0 and isinstance(pair, int):
                        tokens = slice(TOKENS - BANK, TOKENS)
                    dve.wait_ge(down_done, chunks * GROUP)
                    dve.tensor_tensor(x[:, tokens], x[:, tokens], psum[:, DOWN + (j + 1) % 2, :],
                                      ALU.add).then_inc(added, 1)

                def body(k, parity, pair):
                    for j in range(2):
                        for p in range(GROUP):
                            n = unit(k, parity, pair, j, p)
                            dve.wait_ge(silu_ready, n + 1)
                            after(dve, hidden_ready, n - 1)
                            dve.tensor_tensor(gated[:, p % 2, :], silu[:, p % 2, :], psum[:, UP + p % 2, :],
                                              ALU.mult).then_inc(gated_ready, 1)
                            dve.wait_ge(gated_ready, n + 1)
                            dve.wait_ge(mask_spread, n + 1)
                            after(dve, low_ready, n - 1)
                            dve.tensor_tensor(hidden[:, p % 2, :], gated[:, p % 2, :], psum[:, SPREAD + p % 2, :],
                                              ALU.mult).then_inc(hidden_ready, 1)
                            if p == 0 and j == 0 and not isinstance(pair, int):
                                dve.wait_ge(loaded[1 - parity], next_group_loads(k, parity))
                                after(dve, down_done, k * (2 * PER) + parity * PER)
                                dve.tensor_copy(w_hi[:, 1 - parity, ds(pair - 1, 1), :],
                                                raw[:, 1 - parity, ds(pair - 1, 1), :]).then_inc(high_split, 1)
                        add(k, parity, pair, j)

                dve.wait_ge(loaded[0], 16 * PARTS)
                for m in range(PARTS):
                    dve.tensor_copy(w_hi[:, 0, m, :], raw[:, 0, m, :]).then_inc(high_split, 1)
                walk(dve, body)
                add(GROUPS // 2, 0, 0, 0)
                dve.wait_ge(added, GROUPS * CHUNKS)

            @block.gpsimd
            def _(pool):
                def body(k, parity, pair):
                    for j in range(2):
                        for p in range(GROUP):
                            n = unit(k, parity, pair, j, p)
                            pool.wait_ge(high_ready, n + 1)
                            pool.tensor_tensor(lo[:, p, :], hidden[:, p % 2, :], f(hi[:, p, :]),
                                               ALU.subtract).then_inc(low_ready, 1)
                            if p == 0 and j == 1 and not isinstance(pair, int):
                                pool.wait_ge(high_split, k * (2 * PARTS) + pair + PARTS * (parity + 1))
                                pool.tensor_tensor(w_lo[:, 1 - parity, ds(pair - 1, 1), :],
                                                   raw[:, 1 - parity, ds(pair - 1, 1), :],
                                                   f(w_hi[:, 1 - parity, ds(pair - 1, 1), :]),
                                                   ALU.subtract).then_inc(low_split, 1)

                for m in range(PARTS):
                    pool.wait_ge(high_split, m + 1)
                    pool.tensor_tensor(w_lo[:, 0, m, :], raw[:, 0, m, :], f(w_hi[:, 0, m, :]),
                                       ALU.subtract).then_inc(low_split, 1)
                walk(pool, body)


def moe_layer(nc, tag, psum, consts, dram, x):
    with ExitStack() as ctx:
        sb = sb_in(ctx, nc)
        n_hi, n_lo = sb(f"{tag}_n_hi", [P, TOKENS], F32R), sb(f"{tag}_n_lo", [P, TOKENS], F32R)
        mask = sb(f"{tag}_mask", [P, TOKENS], F32R)
        layernorm(nc, f"{tag}_norm", psum, consts, x, n_hi[:, :], n_lo[:, :])
        with ExitStack() as small:
            names = ("router", "shared_gate", "shared_up", "shared_down")
            weights = {name: (sb_in(small, nc)(f"{tag}_{name}_hi", [P, P], F32R),
                              sb_in(small, nc)(f"{tag}_{name}_lo", [P, P], F32R)) for name in names}
            parts = {name: (hi[:, :], lo[:, :]) for name, (hi, lo) in weights.items()}
            load_split(nc, f"{tag}_split", [(dram[name], *parts[name]) for name in names])
            route(nc, f"{tag}_route", psum, consts, parts["router"], n_hi, n_lo, mask)
            shared_expert(nc, f"{tag}_shared", psum, [parts[name] for name in names[1:]], n_hi, n_lo, x)
        experts(nc, f"{tag}_experts", psum, [dram[name] for name in ("gate", "up", "down", "pick")],
                n_hi, n_lo, mask, x)


TRAIL = 5


def head_attention(nc, tag, psum, consts, dram, x):
    with ExitStack() as ctx:
        sb, sem = sb_in(ctx, nc), sems_in(ctx, nc, tag)
        w_hi, w_lo = sb(f"{tag}_w_hi", [P, HEADS * P], F32R), sb(f"{tag}_w_lo", [P, HEADS * P], F32R)
        spread = consts["row_spread"]
        load_split(nc, f"{tag}_split", [(dram["head_w"], w_hi[:, :], w_lo[:, :])])

        high_dram = nc.dram_tensor(f"{tag}_high", (P, TOKENS), F32, kind="Internal").ap()
        low_dram = nc.dram_tensor(f"{tag}_low", (P, TOKENS), F32, kind="Internal").ap()
        heads_dram = nc.dram_tensor(f"{tag}_heads", (HEADS * 2 * HEAD, TOKENS), F32, kind="Internal").ap()
        written = sem("written")
        with ExitStack() as first:
            sb_first = sb_in(first, nc)
            n_hi, n_lo = sb_first(f"{tag}_n_hi", [P, TOKENS], F32R), sb_first(f"{tag}_n_lo", [P, TOKENS], F32R)
            layernorm(nc, f"{tag}_norm", psum, consts, x, n_hi[:, :], n_lo[:, :])
            with nc.Block() as block:
                def write(eng, part, whole, n):
                    eng.dma_start(whole, f(n[:, :])).then_inc(written, 16)
                    for h in range(HEADS):
                        eng.dma_start(heads_dram[h * 16 + part * 8:h * 16 + part * 8 + 8, :],
                                      f(n[h * 8:h * 8 + 8, :])).then_inc(written, 16)
                    eng.wait_ge(written, 16 * 2 * (HEADS + 1))

                @block.sync
                def _(sp):
                    write(sp, 0, high_dram, n_hi)

                @block.scalar
                def _(act):
                    write(act, 1, low_dram, n_lo)

        left = sb(f"{tag}_left", [P, 2, T], F32R)
        right = sb(f"{tag}_right", [P, 2, T], F32R)
        row_hi, row_lo = sb(f"{tag}_row_hi", [P, 2, T], F32R), sb(f"{tag}_row_lo", [P, 2, T], F32R)
        v_hi, v_lo = sb(f"{tag}_v_hi", [P, 2, TILES, 2, P], F32R), sb(f"{tag}_v_lo", [P, 2, TILES, 2, P], F32R)
        e = sb(f"{tag}_e", [P, 4, T])
        e_hi, e_lo = sb(f"{tag}_e_hi", [P, TILES, T], F32R), sb(f"{tag}_e_lo", [P, TILES, T], F32R)
        half_sums = sb(f"{tag}_half_sums", [P, 2, HALVES, TILES])
        sums = sb(f"{tag}_sums", [P, TILES])
        inverse = sb(f"{tag}_inverse", [P, 2, 32])
        inverse_rows = sb(f"{tag}_inverse_rows", [2 * 32, P], F32R)
        scale = sb(f"{tag}_scale", [P, HALVES, BANK])
        scaled = sb(f"{tag}_scaled", [P, HALVES, BANK])
        SCORES, OUT, ROWS, VALUES = 0, 2, 6, 7

        quads_loaded = [sem("quads_even"), sem("quads_odd")]
        rows_loaded = [sem("rows_even"), sem("rows_odd")]
        scores_done, exp_done, e_high, low_even, low_odd = (
            sem("scores"), sem("exp"), sem("e_high"), sem("low_even"), sem("low_odd"))
        out_done, v_done, v_high, v_low = sem("out"), sem("v"), sem("v_high"), sem("v_low")
        inverse_ready, turned, rows_high, rows_ready = sem("inverse"), sem("turned"), sem("rows_high"), sem("rows")
        spread_done, scale_ready, scaled_ready, added = sem("spread"), sem("scale"), sem("scaled"), sem("added")
        passed, pe_passed, pool_passed, inverse_clear, sums_ready = sem("passed"), sem("pe_passed"), sem("pool_passed"), sem("inverse_clear"), sem("sums")
        QUAD_LOADS, ROW_LOADS = 5 * QUAD, 2
        VALUE_STEPS = (5, 7)
        ITERATIONS = BATCH * HEADS // (2 * QUAD)

        def walk(eng, step):
            def two_quads(it):
                for parity in range(2):
                    for j in range(QUAD):
                        for s in range(TILES):
                            step(it, parity, j, s)
            two_quads(0)
            with eng.Fori(1, ITERATIONS) as it:
                two_quads(it)

        def head(it, parity, j):
            return it * (2 * QUAD) + (parity * QUAD + j)

        def number(it, parity, j, s):
            return it * (2 * QUAD * TILES) + ((parity * QUAD + j) * TILES + s)

        def none_before(it, parity, j):
            return isinstance(it, int) and it == 0 and parity == 0 and j == 0

        def low_sem(s):
            return low_odd if s % 2 else low_even

        def low_count(it, parity, j, s):
            return it * (QUAD * TILES) + ((parity * QUAD + j) * TILES + s) // 2 + 1

        def piece(it, parity, j, s):
            return it * 16 + (parity * 8 + j * 2 + (s == VALUE_STEPS[1])) + 5

        with nc.Block() as block:
            @block.sync
            def _(sp):
                def load_rows(it, parity):
                    at = ds((it // 2) * T, T)
                    sp.dma_start(f(row_hi[:, parity, :]), high_dram[:, at]).then_inc(rows_loaded[parity], 16)
                    sp.dma_start(f(row_lo[:, parity, :]), low_dram[:, at]).then_inc(rows_loaded[parity], 16)

                def free(it, parity):
                    count = it * (2 * QUAD * TILES * HALVES) + (parity - 1) * (QUAD * TILES * HALVES)
                    if isinstance(count, int):
                        after(sp, scores_done, count)
                    else:
                        wait_apart(sp, scores_done, count, passed)

                def load(it, parity):
                    free(it, parity)
                    load_rows(it, parity)
                    at = ds((it // 2) * T, T)
                    for j in range(QUAD):
                        row = (it % 2) * (2 * QUAD * 16) + (parity * QUAD + j) * 16
                        whole, high, low = (heads_dram[ds(row, 16), at], heads_dram[ds(row, 8), at],
                                            heads_dram[ds(row + 8, 8), at])
                        to = 32 * j
                        for tile, start, source in ((left, 0, whole), (right, 0, whole), (left, 16, whole),
                                                    (right, 16, low), (right, 24, high)):
                            sp.dma_start(f(tile[to + start:to + start + source.shape[0], parity, :]),
                                         source).then_inc(quads_loaded[parity], 16)

                for parity in range(2):
                    load(0, parity)
                with sp.Fori(1, ITERATIONS) as it:
                    for parity in range(2):
                        load(it, parity)
                free(ITERATIONS, 0)
                load_rows(0, 0)

            @block.tensor
            def _(pe):
                def values(it, parity, jp, piece_count, i):
                    after(pe, v_low, piece_count - 1)
                    cols = ds((it % 2) * (2 * QUAD * P) + (parity * QUAD + jp * 2) * P, 2 * P)
                    for v in (2 * i, 2 * i + 1):
                        tile = slice(v * P, (v + 1) * P)
                        last = product(pe, psum[:, VALUES, (v % 2) * 2 * P:(v % 2 + 1) * 2 * P],
                                       (row_hi[:, parity, tile], row_lo[:, parity, tile]),
                                       (w_hi[:, cols], w_lo[:, cols]))
                    last.then_inc(v_done, 1)

                def step(it, parity, j, s, tail=False):
                    n = number(it, parity, j, s)
                    h = head(it, parity, j)
                    started = not (isinstance(n, int) and n < TRAIL) and not (tail and s >= TRAIL)
                    ps, pj = (s - TRAIL) % TILES, (j - (s < TRAIL)) % QUAD
                    if not tail and j == 0 and s == 0:
                        pe.wait_ge(quads_loaded[parity], it * (16 * QUAD_LOADS) + 16 * QUAD_LOADS)
                    for half in range(HALVES):
                        at = slice(half * BANK, (half + 1) * BANK)
                        if not tail:
                            rows = slice(32 * j, 32 * j + 32)
                            after(pe, exp_done, n * HALVES + (half - 1))
                            pe.matmul(psum[:, SCORES + half, :], left[rows, parity, s * P:(s + 1) * P],
                                      right[rows, parity, at], start=True, stop=True).then_inc(scores_done, 1)
                        if started:
                            if half == 0:
                                if ps == 0:
                                    after(pe, scaled_ready, (h - 1) * HALVES)
                                    if j % 2 == 0:
                                        pe.wait_ge(v_low, piece(it, parity, j, 0) - 1)
                                pe.wait_ge(low_sem(ps), low_count(it, parity, j, s - TRAIL))
                            v = (slice(None), (pj // 2) % 2, ps, pj % 2, slice(None))
                            last = product(pe, psum[:, OUT + HALVES * (pj % 2) + half, :], (v_hi[v], v_lo[v]),
                                           (e_hi[:, ps, at], e_lo[:, ps, at]), first=ps == 0, last=ps == TILES - 1)
                    if started:
                        last.then_inc(out_done, 1)
                    if not tail and s in VALUE_STEPS:
                        next_it = it + 1 if parity == 1 and j >= 2 else it
                        next_parity = (parity + (j >= 2)) % 2
                        if s == VALUE_STEPS[0] and j == 2:
                            pe.wait_ge(rows_loaded[next_parity], next_it * (16 * ROW_LOADS) + 16 * ROW_LOADS)
                        values(next_it, next_parity, (j // 2 + 1) % 2, piece(it, parity, j, s),
                               (j % 2) * 2 + VALUE_STEPS.index(s))
                    if none_before(it, parity, j):
                        return
                    if s == 1:
                        after(pe, scale_ready, (h - 1) * HALVES)
                        if isinstance(h, int):
                            pe.wait_ge(inverse_ready, h)
                        else:
                            wait_apart(pe, inverse_ready, h, pe_passed)
                        pe.transpose(psum[0:64, ROWS, 0:P], inverse[:, :, :].rearrange("p a b -> p (a b)"),
                                     consts["identity"]).then_inc(turned, 1)
                    if s in (3, 5):
                        half = (s - 3) // 2
                        pe.wait_ge(rows_ready, h)
                        if half:
                            pe.wait_ge(scale_ready, (h - 1) * HALVES + 1)
                        for q in range(4):
                            tile = half * 4 + q
                            last = pe.matmul(psum[:, ROWS, q * P:(q + 1) * P], spread[:, tile * P:(tile + 1) * P],
                                             inverse_rows[:, :], start=q == 0, stop=q == 3, skip_group_check=True)
                        last.then_inc(spread_done, 1)

                pe.wait_ge(rows_loaded[0], 16 * ROW_LOADS)
                for i in range(4):
                    values(0, 0, 0, i + 1, i)
                walk(pe, step)
                for s in range(6):
                    step(ITERATIONS, 0, 0, s, tail=True)

            @block.scalar
            def _(act):
                def value_high(slot, i, count, pairs_done):
                    act.wait_ge(v_done, count)
                    after(act, out_done, pairs_done)
                    act.copy(v_hi[:, slot, 2 * i:2 * i + 2, :, :].rearrange("p a b c -> p (a b c)"),
                             psum[:, VALUES, :]).then_inc(v_high, 1)

                def step(it, parity, j, s, tail=False):
                    n = number(it, parity, j, s)
                    h = head(it, parity, j)
                    if not tail:
                        for half in range(HALVES):
                            act.wait_ge(scores_done, n * HALVES + (half + 1))
                            if half == 0:
                                after(act, low_sem(s), low_count(it, parity, j, s) - 2)
                            act.activation(e[:, s % 4, half * BANK:(half + 1) * BANK], psum[:, SCORES + half, :],
                                           ACT.Exp, scale=HEAD ** -0.5,
                                           accum_out=half_sums[:, j % 2, half, s:s + 1]).then_inc(exp_done, 1)
                    if s in VALUE_STEPS and not tail:
                        value_high((j // 2 + 1) % 2, (j % 2) * 2 + VALUE_STEPS.index(s), piece(it, parity, j, s),
                                   it * (2 * QUAD * TILES) + (parity * QUAD + (j // 2) * 2) * TILES)
                    if s in (4, 6) and not none_before(it, parity, j):
                        half = (s - 4) // 2
                        act.wait_ge(spread_done, (h - 1) * HALVES + (half + 1))
                        after(act, scaled_ready, (h - 2) * HALVES + (half + 1))
                        act.copy(scale[:, half, :], psum[:, ROWS, :]).then_inc(scale_ready, 1)

                for i in range(4):
                    value_high(0, i, i + 1, 0)
                walk(act, step)
                for s in (4, 6):
                    step(ITERATIONS, 0, 0, s, tail=True)

            @block.vector
            def _(dve):
                def value_low(slot, i, count):
                    dve.wait_ge(v_high, count)
                    at = v_lo[:, slot, 2 * i:2 * i + 2, :, :].rearrange("p a b c -> p (a b c)")
                    high = v_hi[:, slot, 2 * i:2 * i + 2, :, :].rearrange("p a b c -> p (a b c)")
                    dve.tensor_tensor(at, psum[:, VALUES, :], f(high), ALU.subtract).then_inc(v_low, 1)

                def step(it, parity, j, s, tail=False):
                    n = number(it, parity, j, s)
                    h = head(it, parity, j)
                    before = not none_before(it, parity, j)
                    if s == 0 and before:
                        dve.wait_ge(exp_done, n * HALVES)
                        after(dve, turned, h - 1)
                        dve.tensor_tensor(sums[:, :], half_sums[:, (j - 1) % 2, 0, :], half_sums[:, (j - 1) % 2, 1, :],
                                          ALU.add).then_inc(sums_ready, 1)
                        dve.wait_ge(sums_ready, h)
                        dve.reciprocal(inverse[:, :, 0:TILES],
                                       sums[:, :].unsqueeze(1).to_broadcast([P, 2, TILES])).then_inc(inverse_ready, 1)
                    if not tail:
                        dve.wait_ge(exp_done, n * HALVES + HALVES)
                        after(dve, out_done, n - (TILES - 1))
                        dve.tensor_copy(e_hi[:, s, :], e[:, s % 4, :]).then_inc(e_high, 1)
                        if s % 2:
                            dve.wait_ge(e_high, n + 1)
                            dve.tensor_tensor(e_lo[:, s, :], e[:, s % 4, :], f(e_hi[:, s, :]),
                                              ALU.subtract).then_inc(low_odd, 1)
                    if s == 2 and before:
                        dve.wait_ge(turned, h)
                        after(dve, spread_done, (h - 1) * HALVES)
                        dve.tensor_copy(inverse_rows[:, :], psum[0:64, ROWS, 0:P]).then_inc(rows_high, 1)
                        dve.wait_ge(rows_high, h)
                        dve.tensor_tensor(inverse_rows[32:64, :], psum[32:64, ROWS, 0:P], f(inverse_rows[32:64, :]),
                                          ALU.subtract).then_inc(rows_ready, 1)
                    if s in VALUE_STEPS and not tail:
                        value_low((j // 2 + 1) % 2, (j % 2) * 2 + VALUE_STEPS.index(s), piece(it, parity, j, s))
                    if s == 6 and before:
                        for half in range(HALVES):
                            dve.wait_ge(out_done, h * TILES)
                            dve.wait_ge(scale_ready, (h - 1) * HALVES + half + 1)
                            after(dve, added, (h - 2) * HALVES + half + 1)
                            dve.tensor_tensor(scaled[:, half, :], scale[:, half, :],
                                              psum[:, OUT + HALVES * ((j - 1) % 2) + half, :],
                                              ALU.mult).then_inc(scaled_ready, 1)

                dve.memset(inverse[:, :, :], 0.0).then_inc(inverse_clear, 1)
                dve.wait_ge(inverse_clear, 1)
                for i in range(4):
                    value_low(0, i, i + 1)
                walk(dve, step)
                for s in (0, 2, 6):
                    step(ITERATIONS, 0, 0, s, tail=True)

            @block.gpsimd
            def _(pool):
                def step(it, parity, j, s, tail=False):
                    n = number(it, parity, j, s)
                    h = head(it, parity, j)
                    if s % 2 == 0 and not tail:
                        pool.wait_ge(e_high, n + 1)
                        pool.tensor_tensor(e_lo[:, s, :], e[:, s % 4, :], f(e_hi[:, s, :]),
                                           ALU.subtract).then_inc(low_even, 1)
                    if s == 7 and not none_before(it, parity, j):
                        row = it // 2
                        if parity == 0 and j == 0:
                            row = (it - 1) // 2
                        for half in range(HALVES):
                            at = ds(row * T + half * BANK, BANK)
                            wait_apart(pool, scaled_ready, (h - 1) * HALVES + half + 1, pool_passed)
                            pool.tensor_tensor(x[:, at], x[:, at], scaled[:, half, :], ALU.add).then_inc(added, 1)

                walk(pool, step)
                step(ITERATIONS, 0, 0, 7, tail=True)
                pool.wait_ge(added, BATCH * HEADS * HALVES)



def load_tiles(nc, tag, loads):
    with ExitStack() as ctx:
        loaded = sems_in(ctx, nc, tag)("loaded")
        with nc.Block() as block:
            @block.sync
            def _(sp):
                for tile, source in loads:
                    sp.dma_start(tile, source).then_inc(loaded, 16)
                sp.wait_ge(loaded, 16 * len(loads))


def load_matrices(nc, ctx, tag, dram, names):
    sb = sb_in(ctx, nc)
    tiles = {name: (sb(f"{tag}_{name}_hi", [P, dram[name].shape[1]], F32R),
                    sb(f"{tag}_{name}_lo", [P, dram[name].shape[1]], F32R)) for name in names}
    parts = {name: (hi[:, :], lo[:, :]) for name, (hi, lo) in tiles.items()}
    load_split(nc, f"{tag}_split", [(dram[name], *parts[name]) for name in names])
    return parts


def recurrent_layer(nc, tag, psum, consts, dram, x):
    columns = consts["columns"]
    with ExitStack() as ctx:
        sb, sem = sb_in(ctx, nc), sems_in(ctx, nc, tag)
        n_hi, n_lo = sb(f"{tag}_n_hi", [P, TOKENS], F32R), sb(f"{tag}_n_lo", [P, TOKENS], F32R)
        w = load_matrices(nc, ctx, tag, dram, ("wf", "uf", "wi", "ui", "wc", "uc", "wo", "uo"))
        layernorm(nc, f"{tag}_norm", psum, consts, x, n_hi[:, :], n_lo[:, :])
        gates = sb(f"{tag}_gates", [P, HALVES, 3, BANK])
        kept = sb(f"{tag}_kept", [P, HALVES, BANK])
        new = sb(f"{tag}_new", [P, HALVES, BANK])
        cell = sb(f"{tag}_cell", [P, HALVES, BANK])
        c_hi, c_lo = sb(f"{tag}_c_hi", [P, HALVES, BANK], F32R), sb(f"{tag}_c_lo", [P, HALVES, BANK], F32R)
        h = sb(f"{tag}_h", [P, HALVES, BANK])
        sums_ready, gates_ready, kept_ready, new_ready = sem("sums"), sem("gates"), sem("kept"), sem("new")
        cell_ready, high_ready, low_ready = sem("cell"), sem("high"), sem("low")
        out_ready, h_ready, added = sem("out"), sem("h"), sem("added")
        OUT = 6

        with nc.Block() as block:
            @block.tensor
            def _(pe):
                with pe.Fori(0, BATCH) as t:
                    for half in range(HALVES):
                        at = ds(t * T + half * BANK, BANK)
                        for gate, (wn, un) in enumerate((("wf", "uf"), ("wi", "ui"), ("wc", "uc"))):
                            product(pe, psum[:, half * 3 + gate, :], w[wn], (n_hi[:, at], n_lo[:, at]), last=False)
                    for half in range(HALVES):
                        pe.wait_ge(low_ready, t * HALVES + half + 1)
                        for gate, (wn, un) in enumerate((("wf", "uf"), ("wi", "ui"), ("wc", "uc"))):
                            product(pe, psum[:, half * 3 + gate, :], w[un], (c_hi[:, half, :], c_lo[:, half, :]),
                                    first=False).then_inc(sums_ready, 1)
                    pe.wait_ge(gates_ready, t * (3 * HALVES) + 3 * HALVES)
                pe.wait_ge(low_ready, (BATCH + 1) * HALVES)
                with pe.Fori(0, BATCH) as t:
                    for half in range(HALVES):
                        at = ds(t * T + half * BANK, BANK)
                        product(pe, psum[:, OUT + half, :], w["wo"], (n_hi[:, at], n_lo[:, at]), last=False)
                        product(pe, psum[:, OUT + half, :], w["uo"], (c_hi[:, half, :], c_lo[:, half, :]),
                                first=False).then_inc(out_ready, 1)
                    pe.wait_ge(h_ready, t * HALVES + HALVES)

            @block.scalar
            def _(act):
                act.wait_ge(cell_ready, HALVES)
                for half in range(HALVES):
                    act.copy(c_hi[:, half, :], cell[:, half, :]).then_inc(high_ready, 1)
                with act.Fori(0, BATCH) as t:
                    for half in range(HALVES):
                        for gate, (func, bias) in enumerate(((ACT.Sigmoid, "bf"), (ACT.Sigmoid, "bi"), (ACT.Tanh, "bc"))):
                            act.wait_ge(sums_ready, t * (3 * HALVES) + half * 3 + gate + 1)
                            act.activation(gates[:, half, gate, :], psum[:, half * 3 + gate, :], func,
                                           bias=columns[bias]).then_inc(gates_ready, 1)
                    for half in range(HALVES):
                        act.wait_ge(cell_ready, t * HALVES + HALVES + half + 1)
                        act.copy(c_hi[:, half, :], cell[:, half, :]).then_inc(high_ready, 1)
                with act.Fori(0, BATCH) as t:
                    for half in range(HALVES):
                        act.wait_ge(out_ready, t * HALVES + half + 1)
                        act.activation(h[:, half, :], psum[:, OUT + half, :], ACT.Tanh, bias=columns["bo"]).then_inc(h_ready, 1)
                    act.wait_ge(added, t * HALVES + HALVES)

            @block.vector
            def _(dve):
                for half in range(HALVES):
                    dve.tensor_copy(cell[:, half, :], columns["in_c"].to_broadcast([P, BANK])).then_inc(cell_ready, 1)
                for half in range(HALVES):
                    dve.wait_ge(high_ready, half + 1)
                    dve.tensor_tensor(c_lo[:, half, :], cell[:, half, :], f(c_hi[:, half, :]), ALU.subtract).then_inc(low_ready, 1)
                with dve.Fori(0, BATCH) as t:
                    for half in range(HALVES):
                        dve.wait_ge(gates_ready, t * (3 * HALVES) + half * 3 + 3)
                        dve.wait_ge(low_ready, t * HALVES + HALVES)
                        dve.tensor_tensor(kept[:, half, :], gates[:, half, 0, :], cell[:, half, :], ALU.mult).then_inc(kept_ready, 1)
                        dve.tensor_tensor(new[:, half, :], gates[:, half, 1, :], gates[:, half, 2, :], ALU.mult).then_inc(new_ready, 1)
                        dve.wait_ge(kept_ready, t * HALVES + half + 1)
                        dve.wait_ge(new_ready, t * HALVES + half + 1)
                        dve.tensor_tensor(cell[:, half, :], kept[:, half, :], new[:, half, :], ALU.add).then_inc(cell_ready, 1)
                    for half in range(HALVES):
                        dve.wait_ge(high_ready, t * HALVES + HALVES + half + 1)
                        dve.tensor_tensor(c_lo[:, half, :], cell[:, half, :], f(c_hi[:, half, :]), ALU.subtract).then_inc(low_ready, 1)
                with dve.Fori(0, BATCH) as t:
                    for half in range(HALVES):
                        at = ds(t * T + half * BANK, BANK)
                        dve.wait_ge(h_ready, t * HALVES + half + 1)
                        dve.scalar_tensor_tensor(out=x[:, at], in0=h[:, half, :], scalar=0.5, in1=x[:, at],
                                                 op0=ALU.mult, op1=ALU.add).then_inc(added, 1)
                dve.wait_ge(added, BATCH * HALVES)


def decayed_attention(nc, tag, psum, consts, w, tables, xn, residual):
    columns, inv, causal, ones = consts["columns"], consts["inv"], consts["causal"], consts["ones"]
    (n_hi, n_lo), (cosines, sines) = xn, tables
    with ExitStack() as ctx:
        sb, sem = sb_in(ctx, nc), sems_in(ctx, nc, tag)
        row_hi, row_lo = sb(f"{tag}_row_hi", [P, T], F32R), sb(f"{tag}_row_lo", [P, T], F32R)
        names = ("decay", "decay_log", "decay_max", "clock", "clock_log", "clock_max", "logit", "gain",
                 "total", "rotated", "swapped", "norm")
        tile = {name: sb(f"{tag}_{name}", [P, T])[:, :] for name in names}
        zeros = sb(f"{tag}_zeros", [P, T])[:, :]
        q, k, v = ([sb(f"{tag}_{name}_{part}", [P, T], F32R) for part in ("hi", "lo")] for name in "qkv")
        e = [tile[name] for name in ("decay_log", "decay_max", "clock")]
        inverse, out = (tile[name].rearrange("p (a b) -> p a b", a=HALVES) for name in ("clock_log", "clock_max"))
        e_hi, e_lo = sb(f"{tag}_e_hi", [P, 3, T], F32R), sb(f"{tag}_e_lo", [P, 3, T], F32R)
        top = sb(f"{tag}_top", [P, 1])[:, :]
        products = {name: sem(f"p_{name}") for name in ("gate", "logit", "clock", "q", "q_swap", "q_square",
                                                        "k", "k_swap", "k_square", "v")}
        rows_loaded, cleared, sp_passed = sem("rows_loaded"), sem("cleared"), sem("sp_passed")
        abs_ready, exp_ready, log_ready, max_ready = ({kind: sem(f"{step}_{kind}") for kind in ("decay", "clock")}
                                                      for step in ("abs", "exp", "log", "max"))
        decay_sum, decay_clipped, decay_ready, clock_ready = sem("decay_sum"), sem("decay_clipped"), sem("decay"), sem("clock")
        logit_ready, top_ready, gain_exp, gain_ready, total_ready = (
            sem("logit"), sem("top"), sem("gain_exp"), sem("gain"), sem("total"))
        per_side = ("square", "norm_root", "norm_floor", "norm", "norm_inverse", "cosine", "sine", "rotated", "weighted", "ready", "high", "low")
        side = {name: {step: sem(f"{name}_{step}") for step in per_side} for name in ("q", "k")}
        v_high, v_low = sem("v_high"), sem("v_low")
        GATE, LOGIT, CLOCK, QUERY = 0, 2, 4, 6

        def pair(base):
            return psum[:, base:base + 2, :].rearrange("p a b -> p (a b)")

        banks = {"q": (QUERY, GATE, LOGIT), "k": (CLOCK, GATE, LOGIT)}

        scores_done, masked, exp_done, e_high, e_low = sem("scores"), sem("masked"), sem("exp"), sem("e_high"), sem("e_low")
        out_done, inverse_ready, out_ready, added = sem("out_done"), sem("inverse"), sem("out"), sem("added")
        SCORES, OUT, SUMS = 0, 4, 6
        LATE = 2

        def segments(s):
            first = s * P
            return [(half, max(first - half * BANK, 0), BANK) for half in range(HALVES) if first < (half + 1) * BANK]

        def projected(eng, b):
            for s in (side["q"]["low"], side["k"]["low"], v_low):
                eng.wait_ge(s, b + 1)

        def row_over(eng, b):
            eng.wait_ge(added, b * HALVES + HALVES)

        with nc.Block() as block:
            @block.sync
            def _(sp):
                with sp.Fori(0, BATCH) as b:
                    sp.dma_start(f(row_hi[:, :]), f(n_hi[:, ds(b * T, T)])).then_inc(rows_loaded, 16)
                    sp.dma_start(f(row_lo[:, :]), f(n_lo[:, ds(b * T, T)])).then_inc(rows_loaded, 16)
                    wait_apart(sp, added, b * HALVES + HALVES, sp_passed)

            @block.tensor
            def _(pe):
                with pe.Fori(0, BATCH) as b:
                    def project(name, base):
                        for half in range(HALVES):
                            at = ds(b * T + half * BANK, BANK)
                            last = product(pe, psum[:, base + half, :], w[name], (n_hi[:, at], n_lo[:, at]))
                        last.then_inc(products[name], 1)

                    def square(name, base):
                        pe.wait_ge(side[name]["square"], b + 1)
                        for half in range(HALVES):
                            last = pe.matmul(psum[:, base + half, :], inv, tile["norm"][:, half * BANK:(half + 1) * BANK],
                                             start=True, stop=True)
                        last.then_inc(products[f"{name}_square"], 1)

                    project("gate", GATE)
                    project("logit", LOGIT)
                    project("clock", CLOCK)
                    project("q", QUERY)
                    pe.wait_ge(max_ready["decay"], b + 1)
                    pe.wait_ge(abs_ready["decay"], b + 1)
                    project("q_swap", GATE)
                    pe.wait_ge(logit_ready, b + 1)
                    square("q", LOGIT)
                    pe.wait_ge(max_ready["clock"], b + 1)
                    pe.wait_ge(abs_ready["clock"], b + 1)
                    project("k", CLOCK)
                    pe.wait_ge(side["q"]["sine"], b + 1)
                    project("k_swap", GATE)
                    pe.wait_ge(side["q"]["norm_root"], b + 1)
                    square("k", LOGIT)
                    pe.wait_ge(side["q"]["cosine"], b + 1)
                    pe.wait_ge(rows_loaded, b * 32 + 32)
                    for s in range(TILES):
                        at = slice(s * P, (s + 1) * P)
                        last = product(pe, psum[:, QUERY + s // 4, (s % 4) * P:(s % 4 + 1) * P],
                                       (row_hi[:, at], row_lo[:, at]), w["v_out"])
                    last.then_inc(products["v"], 1)
                    projected(pe, b)

                    for s in range(TILES + LATE):
                        if s < TILES:
                            at = slice(s * P, (s + 1) * P)
                            if s >= 2:
                                pe.wait_ge(exp_done, b * TILES + (s - 1))
                            for half, first, end in segments(s):
                                queries = slice(half * BANK + first, half * BANK + end)
                                last = product(pe, psum[:, SCORES + 2 * (s % 2) + half, first:end],
                                               (k[0][:, at], k[1][:, at]), (q[0][:, queries], q[1][:, queries]))
                            last.then_inc(scores_done, 1)
                        if s >= LATE:
                            p = s - LATE
                            at = slice(p * P, (p + 1) * P)
                            pe.wait_ge(e_low, b * TILES + (p + 1))
                            for half, first, end in segments(p):
                                cols = slice(half * BANK + first, half * BANK + end)
                                final = p == (half + 1) * (TILES // HALVES) - 1
                                product(pe, psum[:, OUT + half, first:end], (v[0][:, at], v[1][:, at]),
                                        (e_hi[:, p % 3, cols], e_lo[:, p % 3, cols]), first=p == 0, last=final)
                                pe.matmul(psum[:, SUMS + half, first:end], ones, e_lo[:, p % 3, cols],
                                          start=p == 0, stop=False, skip_group_check=True)
                                last = pe.matmul(psum[:, SUMS + half, first:end], ones, e_hi[:, p % 3, cols],
                                                 start=False, stop=final, skip_group_check=True)
                            last.then_inc(out_done, 1)
                    row_over(pe, b)

            @block.scalar
            def _(act):
                with act.Fori(0, BATCH) as b:
                    for kind, base, bias in (("decay", GATE, "gate_b"), ("clock", CLOCK, "clock_b")):
                        act.wait_ge(products["gate" if kind == "decay" else "clock"], b + 1)
                        act.activation(tile[kind], pair(base), ACT.Abs, bias=columns[bias]).then_inc(abs_ready[kind], 1)
                        act.wait_ge(abs_ready[kind], b + 1)
                        act.activation(tile[kind], tile[kind], ACT.Exp, scale=-1.0).then_inc(exp_ready[kind], 1)
                        act.wait_ge(exp_ready[kind], b + 1)
                        act.activation(tile[f"{kind}_log"], tile[kind], ACT.Ln, bias=columns["one"]).then_inc(log_ready[kind], 1)
                    act.wait_ge(products["q"], b + 1)
                    act.activation(tile["norm"], pair(QUERY), ACT.Square).then_inc(side["q"]["square"], 1)
                    act.wait_ge(top_ready, b + 1)
                    act.activation(tile["gain"], tile["logit"], ACT.Exp, bias=top).then_inc(gain_exp, 1)
                    act.wait_ge(decay_clipped, b + 1)
                    act.activation(tile["decay"], tile["decay"], ACT.Exp, scale=-1.0).then_inc(decay_ready, 1)

                    def norm(name):
                        act.wait_ge(products[f"{name}_square"], b + 1)
                        act.activation(tile["norm"], pair(banks[name][2]), ACT.Sqrt, scale=float(P)).then_inc(side[name]["norm_root"], 1)

                    def high(name, target):
                        act.wait_ge(side[name]["ready"], b + 1)
                        act.copy(target[0][:, :], tile["rotated"]).then_inc(side[name]["high"], 1)

                    norm("q")
                    high("q", q)
                    act.wait_ge(products["k"], b + 1)
                    act.activation(tile["norm"], pair(CLOCK), ACT.Square).then_inc(side["k"]["square"], 1)
                    norm("k")
                    act.wait_ge(products["v"], b + 1)
                    act.copy(v[0][:, :], pair(QUERY)).then_inc(v_high, 1)
                    high("k", k)

                    for s in range(TILES):
                        first = s * P
                        act.wait_ge(masked, b * TILES + (s + 1))
                        if s >= 3:
                            act.wait_ge(e_low, b * TILES + (s - 2))
                        wide = psum[:, SCORES + 2 * (s % 2):SCORES + 2 * (s % 2) + 2, :].rearrange("p a b -> p (a b)")
                        act.activation(e[s % 3][:, first:T], wide[:, first:T], ACT.Exp, scale=float(P) ** -0.5).then_inc(exp_done, 1)
                        act.wait_ge(exp_done, b * TILES + (s + 1))
                        if s >= 3:
                            act.wait_ge(out_done, b * TILES + (s - 2))
                        act.copy(e_hi[:, s % 3, first:T], e[s % 3][:, first:T]).then_inc(e_high, 1)
                    row_over(act, b)

            @block.vector
            def _(dve):
                dve.memset(zeros, 0.0).then_inc(cleared, 1)
                dve.wait_ge(cleared, 1)
                with dve.Fori(0, BATCH) as b:
                    def rectified(kind, base, bias):
                        dve.wait_ge(products["gate" if kind == "decay" else "clock"], b + 1)
                        dve.wait_ge(abs_ready[kind], b + 1)
                        dve.tensor_scalar(tile[f"{kind}_max"], pair(base), columns[bias], 0.0, ALU.add,
                                          ALU.max).then_inc(max_ready[kind], 1)

                    def rotate(name):
                        main, swap, _ = banks[name]
                        dve.wait_ge(side[name]["square"], b + 1)
                        dve.tensor_tensor(tile["rotated"], cosines, pair(main), ALU.mult).then_inc(side[name]["cosine"], 1)
                        dve.wait_ge(products[f"{name}_swap"], b + 1)
                        dve.tensor_tensor(tile["swapped"], sines, pair(swap), ALU.mult).then_inc(side[name]["sine"], 1)

                    def finish(name, denominator, factor):
                        s = side[name]
                        dve.wait_ge(s["norm_root"], b + 1)
                        dve.tensor_scalar(tile["norm"], tile["norm"], 1e-12, None, ALU.max).then_inc(s["norm_floor"], 1)
                        dve.wait_ge(s["norm_floor"], b + 1)
                        dve.scalar_tensor_tensor(out=tile["norm"], in0=tile[denominator], scalar=1e-8, in1=tile["norm"],
                                                 op0=ALU.add, op1=ALU.mult).then_inc(s["norm"], 1)
                        dve.wait_ge(s["norm"], b + 1)
                        dve.reciprocal(tile["norm"], tile["norm"]).then_inc(s["norm_inverse"], 1)
                        dve.wait_ge(s["rotated"], b + 1)
                        dve.tensor_tensor(tile["rotated"], tile["rotated"], tile[factor], ALU.mult).then_inc(s["weighted"], 1)
                        dve.wait_ge(s["weighted"], b + 1)
                        dve.wait_ge(s["norm_inverse"], b + 1)
                        dve.tensor_tensor(tile["rotated"], tile["rotated"], tile["norm"], ALU.mult).then_inc(s["ready"], 1)

                    rectified("decay", GATE, "gate_b")
                    dve.wait_ge(products["logit"], b + 1)
                    dve.tensor_scalar(tile["logit"], pair(LOGIT), columns["p_b"], None, ALU.add).then_inc(logit_ready, 1)
                    dve.wait_ge(logit_ready, b + 1)
                    dve.tensor_reduce(top, tile["logit"], mybir.AxisListType.X, ALU.max, negate=True).then_inc(top_ready, 1)
                    dve.wait_ge(log_ready["decay"], b + 1)
                    dve.wait_ge(max_ready["decay"], b + 1)
                    dve.tensor_tensor_scan(tile["decay"], tile["decay_max"], tile["decay_log"], 0.0,
                                           ALU.add, ALU.add).then_inc(decay_sum, 1)
                    dve.wait_ge(decay_sum, b + 1)
                    dve.tensor_scalar(tile["decay"], tile["decay"], 60.0, -50.0, ALU.min, ALU.max).then_inc(decay_clipped, 1)
                    rectified("clock", CLOCK, "clock_b")
                    rotate("q")
                    dve.wait_ge(gain_exp, b + 1)
                    dve.wait_ge(clock_ready, b + 1)
                    dve.tensor_tensor(tile["gain"], tile["gain"], tile["clock"], ALU.mult).then_inc(gain_ready, 1)
                    dve.wait_ge(gain_ready, b + 1)
                    dve.tensor_tensor_scan(tile["total"], tile["gain"], zeros, 0.0, ALU.add, ALU.add).then_inc(total_ready, 1)
                    dve.wait_ge(total_ready, b + 1)
                    dve.wait_ge(decay_ready, b + 1)
                    finish("q", "total", "decay")
                    dve.wait_ge(side["q"]["low"], b + 1)
                    rotate("k")
                    dve.wait_ge(v_high, b + 1)
                    dve.tensor_tensor(v[1][:, :], pair(QUERY), f(v[0][:, :]), ALU.subtract).then_inc(v_low, 1)
                    finish("k", "decay", "gain")

                    for s in range(TILES):
                        half, first = s // 4, (s % 4) * P
                        block_at = psum[:, SCORES + 2 * (s % 2) + half, first:first + P]
                        dve.wait_ge(scores_done, b * TILES + (s + 1))
                        dve.tensor_tensor(block_at, causal, block_at, ALU.add).then_inc(masked, 1)
                    for half in range(HALVES):
                        at = ds(b * T + half * BANK, BANK)
                        dve.wait_ge(out_done, b * TILES + (half + 1) * (TILES // HALVES))
                        dve.reciprocal(inverse[:, half, :], psum[:, SUMS + half, :]).then_inc(inverse_ready, 1)
                        dve.wait_ge(inverse_ready, b * HALVES + half + 1)
                        dve.tensor_tensor(out[:, half, :], inverse[:, half, :], psum[:, OUT + half, :], ALU.mult).then_inc(out_ready, 1)
                        dve.wait_ge(out_ready, b * HALVES + half + 1)
                        dve.scalar_tensor_tensor(out=residual[:, at], in0=out[:, half, :], scalar=columns["out_b"],
                                                 in1=residual[:, at], op0=ALU.add, op1=ALU.add).then_inc(added, 1)
                    row_over(dve, b)

            @block.gpsimd
            def _(pool):
                with pool.Fori(0, BATCH) as b:
                    def sum_rotated(name):
                        pool.wait_ge(side[name]["cosine"], b + 1)
                        pool.wait_ge(side[name]["sine"], b + 1)
                        pool.tensor_tensor(tile["rotated"], tile["rotated"], tile["swapped"], ALU.add).then_inc(side[name]["rotated"], 1)

                    def low(name, target):
                        pool.wait_ge(side[name]["high"], b + 1)
                        pool.tensor_tensor(target[1][:, :], tile["rotated"], f(target[0][:, :]), ALU.subtract).then_inc(side[name]["low"], 1)

                    pool.wait_ge(max_ready["clock"], b + 1)
                    pool.wait_ge(log_ready["clock"], b + 1)
                    pool.tensor_tensor(tile["clock"], tile["clock_max"], tile["clock_log"], ALU.add).then_inc(clock_ready, 1)
                    sum_rotated("q")
                    low("q", q)
                    sum_rotated("k")
                    low("k", k)

                    for s in range(TILES):
                        first = s * P
                        pool.wait_ge(e_high, b * TILES + (s + 1))
                        pool.tensor_tensor(e_lo[:, s % 3, first:T], e[s % 3][:, first:T], f(e_hi[:, s % 3, first:T]),
                                           ALU.subtract).then_inc(e_low, 1)
                    row_over(pool, b)


def mlp_layer(nc, tag, psum, consts, w, h_parts, residual, x):
    columns = consts["columns"]
    h_hi, h_lo = h_parts
    W = 4
    with ExitStack() as ctx:
        sb, sem = sb_in(ctx, nc), sems_in(ctx, nc, tag)
        g = sb(f"{tag}_g", [P, 2, W, BANK])
        g_hi, g_lo = sb(f"{tag}_g_hi", [P, 2, W, BANK], F32R), sb(f"{tag}_g_lo", [P, 2, W, BANK], F32R)
        y = sb(f"{tag}_y", [P, 2, BANK])
        up_ready, gelu_ready, high_ready, low_ready, down_ready = sem("up"), sem("gelu"), sem("high"), sem("low"), sem("down")
        y_ready, added = sem("y"), sem("added")
        with nc.Block() as block:
            @block.tensor
            def _(pe):
                with pe.Fori(0, CHUNKS // 2) as r:
                    for j in range(2):
                        at = ds(r * (2 * BANK) + j * BANK, BANK)
                        for m in range(W):
                            cols = slice(m * P, (m + 1) * P)
                            product(pe, psum[:, j * W + m, :], (w["w1"][0][:, cols], w["w1"][1][:, cols]),
                                    (h_hi[:, at], h_lo[:, at])).then_inc(up_ready, 1)
                    for j in range(2):
                        for m in range(W):
                            cols = slice(m * P, (m + 1) * P)
                            pe.wait_ge(low_ready, r * (2 * W) + (j * W + m + 1))
                            last = product(pe, psum[:, j * W, :], (w["w2"][0][:, cols], w["w2"][1][:, cols]),
                                           (g_hi[:, j, m, :], g_lo[:, j, m, :]), first=m == 0, last=m == W - 1)
                        last.then_inc(down_ready, 1)
                    pe.wait_ge(y_ready, r * 2 + 2)

            @block.scalar
            def _(act):
                with act.Fori(0, CHUNKS // 2) as r:
                    for j in range(2):
                        for m in range(W):
                            n = r * (2 * W) + (j * W + m + 1)
                            act.wait_ge(up_ready, n)
                            act.activation(g[:, j, m, :], psum[:, j * W + m, :], ACT.Gelu,
                                           bias=columns[f"b1_{m}"]).then_inc(gelu_ready, 1)
                            act.wait_ge(gelu_ready, n)
                            act.copy(g_hi[:, j, m, :], g[:, j, m, :]).then_inc(high_ready, 1)
                    act.wait_ge(down_ready, r * 2 + 2)

            @block.vector
            def _(dve):
                with dve.Fori(0, CHUNKS // 2) as r:
                    for j in range(2):
                        for m in range(W):
                            dve.wait_ge(high_ready, r * (2 * W) + (j * W + m + 1))
                            dve.tensor_tensor(g_lo[:, j, m, :], g[:, j, m, :], f(g_hi[:, j, m, :]), ALU.subtract).then_inc(low_ready, 1)
                    for j in range(2):
                        at = ds(r * (2 * BANK) + j * BANK, BANK)
                        dve.wait_ge(down_ready, r * 2 + j + 1)
                        dve.scalar_tensor_tensor(out=y[:, j, :], in0=psum[:, j * W, :], scalar=columns["b2"],
                                                 in1=residual[:, at], op0=ALU.add, op1=ALU.add).then_inc(y_ready, 1)
                        dve.wait_ge(y_ready, r * 2 + j + 1)
                        dve.tensor_tensor(x[:, at], x[:, at], y[:, j, :], ALU.add).then_inc(added, 1)
                    dve.wait_ge(added, r * 2 + 2)


def fold_output(nc, tag, psum, w, v_out):
    with ExitStack() as ctx:
        sem = sems_in(ctx, nc, tag)
        ready, high_ready, low_ready = sem("ready"), sem("high"), sem("low")
        with nc.Block() as block:
            @block.tensor
            def _(pe):
                product(pe, psum[:, 0, 0:P], w["v_turned"], w["out"]).then_inc(ready, 1)

            @block.vector
            def _(dve):
                dve.wait_ge(ready, 1)
                dve.tensor_copy(v_out[0], psum[:, 0, 0:P]).then_inc(high_ready, 1)
                dve.wait_ge(high_ready, 1)
                dve.tensor_tensor(v_out[1], psum[:, 0, 0:P], f(v_out[0]), ALU.subtract).then_inc(low_ready, 1)
                dve.wait_ge(low_ready, 1)


def decayed_attention_layer(nc, tag, psum, consts, dram, x):
    columns = consts["columns"]
    with ExitStack() as ctx:
        sb = sb_in(ctx, nc)
        residual = sb(f"{tag}_residual", [P, TOKENS])
        layernorm(nc, f"{tag}_norm", psum, consts, x, None, None, keep=residual)
        with ExitStack() as attention:
            sb = sb_in(attention, nc)
            n_hi, n_lo = (sb(f"{tag}_n_{part}", [P, TOKENS], F32R) for part in ("hi", "lo"))
            layernorm(nc, f"{tag}_norm1", psum, consts, residual, n_hi[:, :], n_lo[:, :],
                      affine=(columns["ln1_g"], columns["ln1_b"]))
            names = ("gate", "logit", "clock", "q", "q_swap", "k", "k_swap", "v_turned", "out")
            w = load_matrices(nc, attention, f"{tag}_w", {name: dram[f"attn_{name}"] for name in names}, names)
            w["v_out"] = tuple(sb(f"{tag}_v_out_{part}", [P, P], F32R)[:, :] for part in ("hi", "lo"))
            fold_output(nc, f"{tag}_fold", psum, w, w["v_out"])
            tables = [sb(f"{tag}_{name}", [P, T]) for name in ("cosines", "sines")]
            load_tiles(nc, f"{tag}_tables", [(table[:, :], dram[name]) for table, name in zip(tables, ("cosines", "sines"))])
            decayed_attention(nc, f"{tag}_attend", psum, consts, w, [table[:, :] for table in tables],
                              (n_hi, n_lo), residual)
        h_hi, h_lo = (sb_in(ctx, nc)(f"{tag}_h_{part}", [P, TOKENS], F32R) for part in ("hi", "lo"))
        layernorm(nc, f"{tag}_norm2", psum, consts, residual, h_hi[:, :], h_lo[:, :],
                  affine=(columns["ln2_g"], columns["ln2_b"]))
        w = load_matrices(nc, ctx, f"{tag}_mlp_w", dram, ("w1", "w2"))
        mlp_layer(nc, f"{tag}_mlp", psum, consts, w, (h_hi, h_lo), residual, x)


VECTORS = ("gate_b", "p_b", "out_b", "clock_b", "one", "ln1_g", "ln1_b", "ln2_g", "ln2_b", "b2",
           "b1_0", "b1_1", "b1_2", "b1_3", "bf", "bi", "bc", "bo", "in_c")


def build(nc, dram, out):
    with ExitStack() as ctx:
        sb = sb_in(ctx, nc)
        psum = ctx.enter_context(nc.psum_tensor("psum", [P, 8, BANK], F32))
        x = sb("x", [P, TOKENS])
        inv, identity, eps = sb("inv", [P, P]), sb("identity", [P, P]), sb("eps", [P, 1])
        row_spread = sb("row_spread", [2 * 32, 16 * P], F32R)
        causal, ones = sb("causal", [P, P]), sb("ones", [P, P], F32R)
        vectors = sb("vectors", [P, len(VECTORS)])
        load_constants(nc, [(x[:, :], dram["x"]), (inv[:, :], dram["inv"]),
                            (identity[:, :], dram["identity"]), (eps[:, :], dram["eps"]),
                            (causal[:, :], dram["causal"]), (vectors[:, :], dram["vectors"])],
                       [(dram["row_spread"], row_spread[:, :]), (dram["ones"], ones[:, :])])
        consts = {"inv": inv[:, :], "identity": identity[:, :], "eps": eps[:, :], "row_spread": row_spread[:, :],
                  "causal": causal[:, :], "ones": ones[:, :],
                  "columns": {name: vectors[:, i:i + 1] for i, name in enumerate(VECTORS)}}
        moe_layer(nc, "moe0", psum, consts, dram, x)
        head_attention(nc, "heads", psum, consts, dram, x)
        moe_layer(nc, "moe1", psum, consts, dram, x)
        recurrent_layer(nc, "cell0", psum, consts, dram, x)
        decayed_attention_layer(nc, "decay", psum, consts, dram, x)
        recurrent_layer(nc, "cell1", psum, consts, dram, x)
        stored = ctx.enter_context(nc.semaphore("stored"))
        with nc.Block() as block:
            @block.sync
            def _(sp):
                sp.dma_start(out, x[:, :]).then_inc(stored, 16)
                sp.wait_ge(stored, 16)


def kernel(**inputs):
    import numpy as np
    import concourse.bacc as bacc
    from concourse.bass_utils import run_bass_kernel_spmd

    def given(name):
        return np.asarray(inputs[name])

    def twice(a, axis):
        return np.concatenate([a, a], axis=axis)

    experts_up = ("L0_ffn_expert_gate_k", "L0_ffn_expert_up_k")
    gate, up = (given(name).transpose(1, 0, 2).reshape(P, EXPERTS * HIDDEN) for name in experts_up)
    row_expert = np.arange(EXPERTS * HIDDEN) // HIDDEN
    pick = (np.arange(EXPERTS)[:, None] == row_expert[None, :]).astype(np.float32)
    rates = np.exp(-np.arange(P // 2, dtype=np.float32) * np.float32(math.log(10000.0) / (P // 2)))
    angles = np.arange(T, dtype=np.float32)[None, :] * np.repeat(rates, 2)[:, None]
    signs = np.tile(np.float32([-1.0, 1.0]), P // 2)[:, None]
    swapped = np.arange(P) ^ 1
    key, query = np.arange(P)[:, None], np.arange(P)[None, :]
    attn = "L1_attn_"
    vectors = {
        "gate_b": given(attn + "gate_b"), "p_b": given(attn + "p_b"), "out_b": given(attn + "out_b"),
        "clock_b": np.broadcast_to(given(attn + "clock_b"), (P,)), "one": np.ones(P, np.float32),
        "ln1_g": given(attn + "ln1_g"), "ln1_b": given(attn + "ln1_b"),
        "ln2_g": given(attn + "ln2_g"), "ln2_b": given(attn + "ln2_b"), "b2": given(attn + "mlp_b2"),
        **{f"b1_{m}": given(attn + "mlp_b1")[m * P:(m + 1) * P] for m in range(4)},
        **{name: given("L1_ffn_" + name) for name in ("bf", "bi", "bc", "bo", "in_c")},
    }
    arrays = {
        "x": given("L0_attn_x").reshape(TOKENS, P).T,
        "inv": np.full((P, P), 1.0 / P, np.float32),
        "identity": np.eye(P, dtype=np.float32),
        "eps": np.full((P, 1), EPS, np.float32),
        "router": twice(given("L0_ffn_router_w"), 1),
        "shared_gate": twice(given("L0_ffn_shared_gate_w"), 1),
        "shared_up": twice(given("L0_ffn_shared_up_w"), 1),
        "shared_down": twice(given("L0_ffn_shared_down_w"), 0),
        "gate": gate,
        "up": up,
        "down": given("L0_ffn_expert_down_k").reshape(PAIRS, P, P).transpose(1, 0, 2).reshape(P, PAIRS * P),
        "pick": twice(pick, 0),
        "head_w": given("L0_attn_weight").reshape(HEADS, P, P).transpose(1, 0, 2).reshape(P, HEADS * P),
        "row_spread": np.kron(np.tile(np.eye(32, dtype=np.float32)[:, :16], (2, 1)), np.ones((1, P), np.float32)),
        "causal": np.where(query >= key, 0.0, -1e30).astype(np.float32),
        "ones": np.ones((P, P), np.float32),
        "vectors": np.stack([vectors[name] for name in VECTORS], axis=1),
        "cosines": np.cos(angles),
        "sines": np.sin(angles) * signs,
        **{name: given("L1_ffn_" + name).T for name in ("wf", "uf", "wi", "ui", "wc", "uc", "wo", "uo")},
        "attn_gate": given(attn + "gate_W"),
        "attn_logit": given(attn + "p_W"),
        "attn_clock": np.broadcast_to(given(attn + "clock_W"), (P, P)),
        "attn_q": given(attn + "Wq"),
        "attn_q_swap": given(attn + "Wq")[:, swapped],
        "attn_k": given(attn + "Wk"),
        "attn_k_swap": given(attn + "Wk")[:, swapped],
        "attn_v_turned": given(attn + "Wv").T,
        "attn_out": given(attn + "out_W"),
        "w1": given(attn + "mlp_W1"),
        "w2": given(attn + "mlp_W2").reshape(4, P, P).transpose(1, 0, 2).reshape(P, 4 * P),
    }
    arrays = {name: np.ascontiguousarray(a) for name, a in arrays.items()}
    nc = bacc.Bacc("TRN2", target_bir_lowering=False, num_devices=1)
    dram = {name: nc.dram_tensor(f"in_{name}", a.shape, F32, kind="ExternalInput").ap() for name, a in arrays.items()}
    out = nc.dram_tensor("out", (P, TOKENS), F32, kind="ExternalOutput").ap()
    build(nc, dram, out)
    result = run_bass_kernel_spmd(nc, [{f"in_{name}": a for name, a in arrays.items()}], core_ids=[0])
    return result.results[0]["out"].T.reshape(BATCH, T, P)
```

```python
import math
from contextlib import ExitStack

import concourse.bass as bass
from concourse import mybir
from concourse.alu_op_type import AluOpType as ALU

F32 = mybir.dt.float32
F32R = mybir.dt.float32r
ACT = mybir.ActivationFunctionType
ds = bass.ds

P = 128
BATCH, T = 4, 1024
TOKENS = BATCH * T
BANK = 512
CHUNKS = TOKENS // BANK
HALVES = T // BANK
EPS = 1e-5

EXPERTS, HIDDEN, TOP = 64, 64, 8
PAIRS = EXPERTS * HIDDEN // P
GROUP = 4
GROUPS = PAIRS // GROUP
COLS = GROUP * P
PARTS = 3
LAG = 3

HEADS, HEAD = 16, 8
QUAD = 4
TILES = T // P


def sb_in(ctx, nc):
    def sb(name, shape, dt=F32):
        return ctx.enter_context(nc.sbuf_tensor(name, shape, dt))
    return sb


def sems_in(ctx, nc, tag):
    handles = []

    def sem(name):
        handles.append(nc.alloc_semaphore(name=f"{tag}_{name}"))
        return handles[-1]

    def clear():
        nc.clear_and_free_semaphores(handles)
        nc.all_engine_barrier()

    ctx.callback(clear)
    return sem


def after(eng, sem, count):
    if isinstance(count, int) and count <= 0:
        return
    eng.wait_ge(sem, count)


def wait_apart(eng, sem, count, passed):
    eng.wait_ge(sem, count)
    eng.sem_inc(passed, 1)


def f(ap):
    return ap.bitcast(F32)


def each_chunk(eng, step):
    step(0, 0, False)
    step(1, 1, False)
    with eng.Fori(1, CHUNKS // 2 - 1) as r:
        for j in range(2):
            step(r * 2 + j, j, False)
    step(CHUNKS - 2, 0, False)
    step(CHUNKS - 1, 1, True)


def product(pe, out, w, x, first=True, last=True):
    (w_hi, w_lo), (x_hi, x_lo) = w, x
    pe.matmul(out, w_lo, x_hi, start=first, stop=False, skip_group_check=True)
    pe.matmul(out, w_hi, x_lo, start=False, stop=False, skip_group_check=True)
    return pe.matmul(out, w_hi, x_hi, start=False, stop=last, skip_group_check=True)


def load_constants(nc, loads, exact):
    with ExitStack() as ctx:
        sem = sems_in(ctx, nc, "constants")
        loaded, exact_loaded, exact_ready = (sem(name) for name in
                                             ("constants_loaded", "exact_loaded", "exact_ready"))
        raws = [sb_in(ctx, nc)(f"exact_raw{i}", tile.shape) for i, (_, tile) in enumerate(exact)]
        with nc.Block() as block:
            @block.sync
            def _(sp):
                for tile, source in loads:
                    sp.dma_start(tile, source).then_inc(loaded, 16)
                sp.wait_ge(loaded, 16 * len(loads))

            @block.scalar
            def _(act):
                for raw, (source, _) in zip(raws, exact):
                    act.dma_start(raw[:, :], source).then_inc(exact_loaded, 16)

            @block.vector
            def _(dve):
                dve.wait_ge(exact_loaded, 16 * len(exact))
                for raw, (_, tile) in zip(raws, exact):
                    dve.tensor_copy(tile, raw[:, :]).then_inc(exact_ready, 1)
                dve.wait_ge(exact_ready, len(exact))


def matrices(nc, ctx, tag, dram, names):
    sb = sb_in(ctx, nc)
    tiles = {name: (sb(f"{tag}_{name}_hi", [P, dram[name].shape[1]], F32R),
                    sb(f"{tag}_{name}_lo", [P, dram[name].shape[1]], F32R)) for name in names}
    parts = {name: (hi[:, :], lo[:, :]) for name, (hi, lo) in tiles.items()}
    return parts, [(dram[name], *parts[name]) for name in names]


def layernorm(nc, tag, psum, consts, x, n_hi, n_lo, affine=None, keep=None,
              splits=(), loads=(), copies=None, x_dram=None):
    inv, eps, identity, row_pick = consts["inv"], consts["eps"], consts["identity"], consts["row_pick"]
    PARTS_OF_CHUNK = BANK // P
    COLUMNS = TOKENS // P
    RING = 4
    MEAN, SCALE, VARIANCE, TURNED = 0, 2, 6, 7
    VECTOR_LOWS = (2, 5, 7)
    with ExitStack() as ctx:
        sb, sem = sb_in(ctx, nc), sems_in(ctx, nc, tag)
        centered = sb(f"{tag}_centered", [P, CHUNKS, BANK])
        squares = sb(f"{tag}_squares", [P, RING, BANK])
        deviation = sb(f"{tag}_deviation", [P, COLUMNS])
        inverse = sb(f"{tag}_inverse", [P, 2, COLUMNS])
        inverse_rows = sb(f"{tag}_inverse_rows", [2 * COLUMNS, P], F32R)
        normal = sb(f"{tag}_normal", [P, RING, BANK])
        mean_ready, centered_ready, squares_ready = sem("mean"), sem("centered"), sem("squares")
        variance_ready, deviation_ready, inverse_ready, turned = sem("variance"), sem("deviation"), sem("inverse"), sem("turned")
        rows_high, rows_ready, scale_ready, scaled_ready = sem("rows_high"), sem("rows"), sem("scale"), sem("scaled")
        normal_ready = scaled_ready if affine is None else sem("normal")
        high_ready = sem("high")
        low_ready = {"vector": sem("vector_low"), "pool": sem("pool_low")}
        raws = [sb(f"{tag}_raw{i}", [P, hi.shape[1]]) for i, (_, hi, _) in enumerate(splits)]
        raw_loaded = [sem(f"raw_loaded{i}") for i in range(len(splits))]
        tiles_loaded, split_high, split_low = sem("tiles_loaded"), sem("split_high"), sem("split_low")
        copied, x_loaded = sem("copied"), [sem(f"x_loaded{c}") for c in range(CHUNKS if x_dram is not None else 0)]

        def chunk(c):
            return slice(c * BANK, (c + 1) * BANK)

        def take_low(eng, who, c):
            eng.wait_ge(high_ready, c + 1)
            eng.tensor_tensor(n_lo[:, chunk(c)], normal[:, c % RING, :], f(n_hi[:, chunk(c)]),
                              ALU.subtract).then_inc(low_ready[who], 1)

        def wait_low(eng, c):
            who = "vector" if c in VECTOR_LOWS else "pool"
            eng.wait_ge(low_ready[who], sum((i in VECTOR_LOWS) == (c in VECTOR_LOWS) for i in range(c + 1)))

        with nc.Block() as block:
            @block.sync
            def _(sp):
                for c, arrived in enumerate(x_loaded):
                    sp.dma_start(x[:, chunk(c)], x_dram[:, chunk(c)]).then_inc(arrived, 16)
                for raw, (source, _, _), arrived in zip(raws, splits, raw_loaded):
                    sp.dma_start(raw[:, :], source).then_inc(arrived, 16)
                for tile, source in loads:
                    sp.dma_start(tile, source).then_inc(tiles_loaded, 16)
                if copies is not None:
                    for c in range(CHUNKS):
                        wait_low(sp, c)
                        for to, part in zip(copies, (n_hi, n_lo)):
                            sp.dma_start(to[:, chunk(c)], f(part[:, chunk(c)])).then_inc(copied, 16)
                    sp.wait_ge(copied, 16 * 2 * CHUNKS)
                if loads:
                    sp.wait_ge(tiles_loaded, 16 * len(loads))

            @block.tensor
            def _(pe):
                def variance(c):
                    pe.wait_ge(squares_ready, c + 1)
                    for q in range(PARTS_OF_CHUNK):
                        column = c * PARTS_OF_CHUNK + q
                        last = pe.matmul(psum[:, VARIANCE, column:column + 1], squares[:, c % RING, q * P:(q + 1) * P],
                                         inv[:, 0:1], start=column == 0, stop=column == COLUMNS - 1,
                                         skip_group_check=True)
                    last.then_inc(variance_ready, 1)

                for c in range(CHUNKS):
                    if x_loaded:
                        pe.wait_ge(x_loaded[c], 16)
                    after(pe, centered_ready, c - 1)
                    pe.matmul(psum[:, MEAN + c % 2, :], inv, x[:, chunk(c)], start=True, stop=True).then_inc(mean_ready, 1)
                    if c >= 2:
                        variance(c - 2)
                for c in (CHUNKS - 2, CHUNKS - 1):
                    variance(c)
                pe.wait_ge(inverse_ready, 1)
                pe.transpose(psum[0:2 * COLUMNS, TURNED, 0:P], inverse[:, :, :].rearrange("p a b -> p (a b)"),
                             identity).then_inc(turned, 1)
                pe.wait_ge(rows_ready, 1)
                for c in range(CHUNKS):
                    after(pe, scaled_ready, c - RING + 1)
                    for q in range(PARTS_OF_CHUNK):
                        last = pe.matmul(psum[:, SCALE + c % RING, q * P:(q + 1) * P], row_pick(c * PARTS_OF_CHUNK + q),
                                         inverse_rows[:, :], start=q == 0, stop=q == PARTS_OF_CHUNK - 1,
                                         skip_group_check=True)
                    last.then_inc(scale_ready, 1)

            @block.scalar
            def _(act):
                for c in range(CHUNKS):
                    act.wait_ge(centered_ready, c + 1)
                    after(act, variance_ready, c - RING + 1)
                    act.activation(squares[:, c % RING, :], centered[:, c, :], ACT.Square).then_inc(squares_ready, 1)
                act.wait_ge(variance_ready, CHUNKS)
                act.activation(deviation[:, :], psum[:, VARIANCE, 0:COLUMNS], ACT.Sqrt, bias=eps).then_inc(deviation_ready, 1)
                if keep is None:
                    for c in range(CHUNKS):
                        act.wait_ge(normal_ready, c + 1)
                        act.copy(n_hi[:, chunk(c)], normal[:, c % RING, :]).then_inc(high_ready, 1)

            @block.vector
            def _(dve):
                for c in range(CHUNKS):
                    dve.wait_ge(mean_ready, c + 1)
                    dve.tensor_tensor(centered[:, c, :], x[:, chunk(c)], psum[:, MEAN + c % 2, :],
                                      ALU.subtract).then_inc(centered_ready, 1)
                dve.wait_ge(deviation_ready, 1)
                dve.reciprocal(inverse[:, :, :],
                               deviation[:, :].unsqueeze(1).to_broadcast([P, 2, COLUMNS])).then_inc(inverse_ready, 1)
                dve.wait_ge(turned, 1)
                dve.tensor_copy(inverse_rows[:, :], psum[0:2 * COLUMNS, TURNED, 0:P]).then_inc(rows_high, 1)
                dve.wait_ge(rows_high, 1)
                dve.tensor_tensor(inverse_rows[COLUMNS:2 * COLUMNS, :], psum[COLUMNS:2 * COLUMNS, TURNED, 0:P],
                                  f(inverse_rows[COLUMNS:2 * COLUMNS, :]), ALU.subtract).then_inc(rows_ready, 1)
                for c in range(CHUNKS):
                    if keep is None:
                        to = normal[:, c % RING, :]
                        if c >= RING:
                            wait_low(dve, c - RING)
                    else:
                        to = keep[:, chunk(c)]
                    dve.wait_ge(scale_ready, c + 1)
                    dve.tensor_tensor(to, centered[:, c, :], psum[:, SCALE + c % RING, :], ALU.mult).then_inc(scaled_ready, 1)
                    if affine is not None:
                        dve.wait_ge(scaled_ready, c + 1)
                        dve.tensor_scalar(to, to, affine[0], affine[1], ALU.mult, ALU.add).then_inc(normal_ready, 1)
                    if keep is None and c - 1 in VECTOR_LOWS:
                        take_low(dve, "vector", c - 1)
                if keep is None and CHUNKS - 1 in VECTOR_LOWS:
                    take_low(dve, "vector", CHUNKS - 1)

            @block.gpsimd
            def _(pool):
                for i, (raw, (_, hi, lo)) in enumerate(zip(raws, splits)):
                    pool.wait_ge(raw_loaded[i], 16)
                    pool.tensor_copy(hi, raw[:, :]).then_inc(split_high, 1)
                    pool.wait_ge(split_high, i + 1)
                    pool.tensor_tensor(lo, raw[:, :], f(hi), ALU.subtract).then_inc(split_low, 1)
                if keep is None:
                    for c in range(CHUNKS):
                        if c not in VECTOR_LOWS:
                            take_low(pool, "pool", c)


def route_and_share(nc, tag, psum, consts, router, weights, n_hi, n_lo, mask, x):
    identity = consts["identity"]
    gate, up, down = weights
    with ExitStack() as ctx:
        sb, sem = sb_in(ctx, nc), sems_in(ctx, nc, tag)
        affinity = sb(f"{tag}_affinity", [P, 2, BANK])
        best = sb(f"{tag}_best", [P, 2, 4, TOP])
        rest = sb(f"{tag}_rest", [P, 2, 4, EXPERTS])
        chosen = sb(f"{tag}_chosen", [P, 2, 4, EXPERTS])
        total = sb(f"{tag}_total", [P, 2, 4])
        routed = sb(f"{tag}_routed", [P, 2, 4, 2, EXPERTS])
        share = sb(f"{tag}_share", [P, 2, BANK])
        silu = sb(f"{tag}_silu", [P, 2, BANK])
        hidden = sb(f"{tag}_hidden", [P, 2, BANK])
        hi = sb(f"{tag}_hi", [P, 2, BANK], F32R)
        lo = sb(f"{tag}_lo", [P, 2, BANK], F32R)
        logits_ready, affinity_ready, turned, best_found = sem("logits"), sem("affinity"), sem("turned"), sem("best")
        rest_ready, chosen_ready, total_ready, inverse_ready = sem("rest"), sem("chosen"), sem("total"), sem("inverse")
        routed_ready, routed_turned, mask_high, mask_ready = sem("routed"), sem("routed_turned"), sem("mask_high"), sem("mask")
        up_ready, share_ready, silu_ready, hidden_ready = sem("up"), sem("share"), sem("silu"), sem("hidden")
        high_ready, low_ready, down_ready, added = sem("high"), sem("low"), sem("down"), sem("added")
        passed = sem("passed")
        LOGITS, MASK, TURNED, GATE, UP = 0, 1, 2, 4, 6
        DOWN = GATE

        def tokens(c):
            return ds(c * BANK, BANK)

        with nc.Block() as block:
            @block.tensor
            def _(pe):
                def logits(c, j):
                    after(pe, affinity_ready, c)
                    product(pe, psum[:, LOGITS, :], router, (n_hi[:, tokens(c)], n_lo[:, tokens(c)])).then_inc(logits_ready, 1)

                def turn_affinity(c, j):
                    pe.wait_ge(affinity_ready, c + 1)
                    for q in range(4):
                        turn = pe.transpose(psum[:, TURNED + j, q * P:(q + 1) * P],
                                            affinity[:, j, q * P:(q + 1) * P], identity)
                    turn.then_inc(turned, 1)

                def down_product(c, j):
                    pe.wait_ge(low_ready, c + 1)
                    product(pe, psum[:, DOWN + j, :], down, (hi[:, j, :], lo[:, j, :])).then_inc(down_ready, 1)

                def step(c, j, last):
                    if not last:
                        logits(c + 1, 1 - j)
                    after(pe, added, c - 1)
                    product(pe, psum[:, GATE + j, :], gate, (n_hi[:, tokens(c)], n_lo[:, tokens(c)]))
                    product(pe, psum[:, UP + j, :], up, (n_hi[:, tokens(c)], n_lo[:, tokens(c)])).then_inc(up_ready, 1)
                    if not last:
                        turn_affinity(c + 1, 1 - j)
                    if not (isinstance(c, int) and c == 0):
                        down_product(c - 1, 1 - j)
                    after(pe, mask_ready, c)
                    pe.wait_ge(routed_ready, c * 4 + 4)
                    for q in range(4):
                        turn = pe.transpose(psum[:, MASK, q * P:(q + 1) * P],
                                            routed[:, j, q, :, :].rearrange("p a e -> p (a e)"), identity)
                    turn.then_inc(routed_turned, 1)

                logits(0, 0)
                turn_affinity(0, 0)
                each_chunk(pe, step)
                down_product(CHUNKS - 1, 1)

            @block.scalar
            def _(act):
                def affinities(c, j):
                    act.wait_ge(logits_ready, c + 1)
                    after(act, turned, c - 1)
                    act.activation(affinity[:, j, :], psum[:, LOGITS, :], ACT.Sigmoid).then_inc(affinity_ready, 1)

                def step(c, j, last):
                    if not last:
                        affinities(c + 1, 1 - j)
                    act.wait_ge(up_ready, c + 1)
                    after(act, silu_ready, c - 1)
                    act.activation(share[:, j, :], psum[:, GATE + j, :], ACT.Sigmoid).then_inc(share_ready, 1)
                    act.wait_ge(hidden_ready, c + 1)
                    after(act, down_ready, c - 1)
                    act.copy(hi[:, j, :], hidden[:, j, :]).then_inc(high_ready, 1)

                affinities(0, 0)
                each_chunk(act, step)

            @block.vector
            def _(dve):
                def pick(c, j):
                    def scores(q):
                        return psum[:, TURNED + j, q * P:q * P + EXPERTS]

                    wait_apart(dve, turned, c + 1, passed)
                    for q in range(4):
                        dve.max(best[:, j, q, :], scores(q)).then_inc(best_found, 1)
                    for q in range(4):
                        wait_apart(dve, best_found, c * 4 + (q + 1), passed)
                        dve.match_replace(out=rest[:, j, q, :], in_to_replace=best[:, j, q, :],
                                          in_values=scores(q), imm_value=-1.0).then_inc(rest_ready, 1)
                    for q in range(4):
                        dve.wait_ge(rest_ready, c * 4 + (q + 1))
                        dve.scalar_tensor_tensor(out=chosen[:, j, q, :], in0=rest[:, j, q, :], scalar=0.0,
                                                 in1=scores(q), op0=ALU.is_lt, op1=ALU.mult,
                                                 accum_out=total[:, j, q:q + 1]).then_inc(chosen_ready, 1)
                    dve.wait_ge(chosen_ready, c * 4 + 4)
                    dve.tensor_scalar(total[:, j, :], total[:, j, :], 1e-9, 2.0, ALU.add,
                                      ALU.mult).then_inc(total_ready, 1)
                    dve.wait_ge(total_ready, c + 1)
                    dve.reciprocal(total[:, j, :], total[:, j, :]).then_inc(inverse_ready, 1)
                    dve.wait_ge(inverse_ready, c + 1)
                    for q in range(4):
                        dve.tensor_scalar(routed[:, j, q, :, :],
                                          chosen[:, j, q, :].unsqueeze(1).to_broadcast([P, 2, EXPERTS]),
                                          total[:, j, q:q + 1], None, ALU.mult).then_inc(routed_ready, 1)

                def leave(c, j):
                    dve.wait_ge(routed_turned, c + 1)
                    dve.tensor_copy(mask[:, tokens(c)], psum[:, MASK, :]).then_inc(mask_high, 1)
                    dve.wait_ge(mask_high, c + 1)
                    dve.tensor_tensor(mask[EXPERTS:P, tokens(c)], psum[EXPERTS:P, MASK, :],
                                      f(mask[EXPERTS:P, tokens(c)]), ALU.subtract).then_inc(mask_ready, 1)
                    dve.wait_ge(down_ready, c + 1)
                    dve.tensor_tensor(x[:, tokens(c)], x[:, tokens(c)], psum[:, DOWN + j, :], ALU.add).then_inc(added, 1)

                def step(c, j, last):
                    pick(c, j)
                    if not (isinstance(c, int) and c == 0):
                        leave(c - 1, 1 - j)
                    dve.wait_ge(share_ready, c + 1)
                    dve.scalar_tensor_tensor(out=silu[:, j, :], in0=share[:, j, :], scalar=0.25,
                                             in1=psum[:, GATE + j, :], op0=ALU.mult,
                                             op1=ALU.mult).then_inc(silu_ready, 1)
                    dve.wait_ge(silu_ready, c + 1)
                    after(dve, low_ready, c - 1)
                    dve.tensor_tensor(hidden[:, j, :], silu[:, j, :], psum[:, UP + j, :],
                                      ALU.mult).then_inc(hidden_ready, 1)

                each_chunk(dve, step)
                leave(CHUNKS - 1, 1)
                dve.wait_ge(mask_ready, CHUNKS)
                dve.wait_ge(added, CHUNKS)

            @block.gpsimd
            def _(pool):
                def step(c, j, last):
                    pool.wait_ge(high_ready, c + 1)
                    pool.tensor_tensor(lo[:, j, :], hidden[:, j, :], f(hi[:, j, :]), ALU.subtract).then_inc(low_ready, 1)

                each_chunk(pool, step)


def experts(nc, tag, psum, consts, dram, w_hi, w_lo, n_hi, n_lo, mask, x):
    gate_dram, up_dram, down_dram = dram
    PER = CHUNKS * GROUP
    GATE, UP, SPREAD, DOWN = 0, 2, 4, 6
    with ExitStack() as ctx:
        sb, sem = sb_in(ctx, nc), sems_in(ctx, nc, tag)
        raw = sb(f"{tag}_raw", [P, 2, PARTS, COLS])
        pick = sb(f"{tag}_pick", [P, 2, COLS], F32R)
        silu = sb(f"{tag}_silu", [P, 2, BANK])
        gated = sb(f"{tag}_gated", [P, 2, BANK])
        hidden = sb(f"{tag}_hidden", [P, 2, BANK])
        hi = sb(f"{tag}_hi", [P, GROUP, BANK], F32R)
        lo = sb(f"{tag}_lo", [P, GROUP, BANK], F32R)
        loaded = [sem("loaded_even"), sem("loaded_odd")]
        picked, high_split, low_split = sem("picked"), sem("high_split"), sem("low_split")
        up_ready, mask_spread, silu_ready, gated_ready = sem("up"), sem("mask_spread"), sem("silu"), sem("gated")
        hidden_ready, high_ready, low_ready = sem("hidden"), sem("high"), sem("low")
        down_done, added, passed = sem("down"), sem("added"), sem("passed")

        def walk(eng, body):
            def two_groups(k):
                for parity in range(2):
                    body(k, parity, 0)
                    with eng.Fori(1, CHUNKS // 2) as pair:
                        body(k, parity, pair)
            two_groups(0)
            with eng.Fori(1, GROUPS // 2) as k:
                two_groups(k)

        def unit(k, parity, pair, j, p):
            return k * (2 * PER) + pair * (2 * GROUP) + (parity * PER + j * GROUP + p)

        def next_group_loads(k, parity):
            return k * (16 * PARTS) + 16 * PARTS * (1 + parity)

        with nc.Block() as block:
            @block.sync
            def _(sp):
                def load(k, parity, source_group):
                    splits = k * (2 * PARTS) + PARTS * (parity - 1)
                    if isinstance(splits, int):
                        after(sp, low_split, splits)
                    else:
                        wait_apart(sp, low_split, splits, passed)
                    for m, source in enumerate((gate_dram, up_dram, down_dram)):
                        sp.dma_start(raw[:, parity, m, :],
                                     source[:, ds(source_group * COLS, COLS)]).then_inc(loaded[parity], 16)

                sp.sem_inc(loaded[0], 16 * PARTS)
                load(0, 1, 1)
                with sp.Fori(1, GROUPS // 2) as k:
                    for parity in range(2):
                        load(k, parity, k * 2 + parity)
                load(GROUPS // 2, 0, 0)

            @block.tensor
            def _(pe):
                def down(k, parity, pair, j, p):
                    m, pm = unit(k, parity, pair, j, p) - LAG, (p - LAG) % GROUP
                    chunk_before = p < LAG
                    group_before = chunk_before and j == 0 and isinstance(pair, int)
                    w_at = 1 - parity if group_before else parity
                    bank = DOWN + ((j + 1) % 2 if chunk_before else j)
                    if isinstance(m, int) and m < 0:
                        return
                    pe.wait_ge(low_ready, m + 1)
                    if pm == 0:
                        count = (k * (2 * CHUNKS) + pair * 2) + (parity * CHUNKS + j - chunk_before - 1)
                        after(pe, added, count)
                    cols = slice(pm * P, (pm + 1) * P)
                    product(pe, psum[:, bank, :], (w_hi[:, w_at, 2, cols], w_lo[:, w_at, 2, cols]),
                            (hi[:, pm, :], lo[:, pm, :]), first=pm == 0, last=pm == GROUP - 1).then_inc(down_done, 1)

                def body(k, parity, pair):
                    if isinstance(pair, int):
                        pe.wait_ge(low_split, k * (2 * PARTS) + PARTS * (parity + 1))
                        pe.wait_ge(picked, k * 2 + (parity + 1))
                    for j in range(2):
                        tokens = ds(pair * (2 * BANK) + j * BANK, BANK)
                        n_pair = (n_hi[:, tokens], n_lo[:, tokens])
                        for p in range(GROUP):
                            n = unit(k, parity, pair, j, p)
                            cols = slice(p * P, (p + 1) * P)
                            after(pe, gated_ready, n - 1)
                            product(pe, psum[:, GATE + p % 2, :], (w_hi[:, parity, 0, cols], w_lo[:, parity, 0, cols]), n_pair)
                            product(pe, psum[:, UP + p % 2, :], (w_hi[:, parity, 1, cols], w_lo[:, parity, 1, cols]),
                                    n_pair).then_inc(up_ready, 1)
                            after(pe, hidden_ready, n - 1)
                            pe.matmul(psum[:, SPREAD + p % 2, :], pick[:, parity, cols], mask[:, tokens],
                                      start=True, stop=True).then_inc(mask_spread, 1)
                            down(k, parity, pair, j, p)

                walk(pe, body)
                for p in range(LAG):
                    down(GROUPS // 2, 0, 0, 0, p)

            @block.scalar
            def _(act):
                def high(n, p):
                    act.wait_ge(hidden_ready, n + 1)
                    after(act, down_done, n - (GROUP - 1))
                    act.copy(hi[:, p, :], hidden[:, p % 2, :]).then_inc(high_ready, 1)

                def body(k, parity, pair):
                    for j in range(2):
                        for p in range(GROUP):
                            n = unit(k, parity, pair, j, p)
                            act.wait_ge(up_ready, n + 1)
                            after(act, gated_ready, n - 1)
                            act.activation(silu[:, p % 2, :], psum[:, GATE + p % 2, :], ACT.Silu).then_inc(silu_ready, 1)
                            if not isinstance(n, int) or n > 0:
                                high(n - 1, (p - 1) % GROUP)

                walk(act, body)
                high(GROUPS * PER - 1, GROUP - 1)

            @block.vector
            def _(dve):
                def pick_group(group, at):
                    dve.tensor_copy(pick[:, at, :].rearrange("p (a b) -> p a b", b=HIDDEN),
                                    consts["expert_rows"][:, ds(group * (2 * GROUP), 2 * GROUP)].unsqueeze(2)
                                    .to_broadcast([P, 2 * GROUP, HIDDEN])).then_inc(picked, 1)

                def add(k, parity, pair, j):
                    chunks = (k * (2 * CHUNKS) + pair * 2) + (parity * CHUNKS + j)
                    if isinstance(chunks, int) and chunks <= 0:
                        return
                    tokens = ds(pair * (2 * BANK) + (j - 1) * BANK, BANK)
                    if j == 0 and isinstance(pair, int):
                        tokens = slice(TOKENS - BANK, TOKENS)
                    dve.wait_ge(down_done, chunks * GROUP)
                    dve.tensor_tensor(x[:, tokens], x[:, tokens], psum[:, DOWN + (j + 1) % 2, :],
                                      ALU.add).then_inc(added, 1)

                def body(k, parity, pair):
                    if isinstance(pair, int):
                        after(dve, mask_spread, k * (2 * PER) + parity * PER)
                        pick_group(k * 2 + (parity + 1), 1 - parity)
                    for j in range(2):
                        for p in range(GROUP):
                            n = unit(k, parity, pair, j, p)
                            dve.wait_ge(silu_ready, n + 1)
                            after(dve, hidden_ready, n - 1)
                            dve.tensor_tensor(gated[:, p % 2, :], silu[:, p % 2, :], psum[:, UP + p % 2, :],
                                              ALU.mult).then_inc(gated_ready, 1)
                            dve.wait_ge(gated_ready, n + 1)
                            dve.wait_ge(mask_spread, n + 1)
                            after(dve, low_ready, n - 1)
                            dve.tensor_tensor(hidden[:, p % 2, :], gated[:, p % 2, :], psum[:, SPREAD + p % 2, :],
                                              ALU.mult).then_inc(hidden_ready, 1)
                            if p == 0 and j == 0 and not isinstance(pair, int):
                                dve.wait_ge(loaded[1 - parity], next_group_loads(k, parity))
                                after(dve, down_done, k * (2 * PER) + parity * PER)
                                dve.tensor_copy(w_hi[:, 1 - parity, ds(pair - 1, 1), :],
                                                raw[:, 1 - parity, ds(pair - 1, 1), :]).then_inc(high_split, 1)
                        add(k, parity, pair, j)

                pick_group(0, 0)
                dve.sem_inc(high_split, PARTS)
                walk(dve, body)
                add(GROUPS // 2, 0, 0, 0)
                dve.wait_ge(added, GROUPS * CHUNKS)

            @block.gpsimd
            def _(pool):
                def body(k, parity, pair):
                    for j in range(2):
                        for p in range(GROUP):
                            n = unit(k, parity, pair, j, p)
                            pool.wait_ge(high_ready, n + 1)
                            pool.tensor_tensor(lo[:, p, :], hidden[:, p % 2, :], f(hi[:, p, :]),
                                               ALU.subtract).then_inc(low_ready, 1)
                            if p == 0 and j == 1 and not isinstance(pair, int):
                                pool.wait_ge(high_split, k * (2 * PARTS) + pair + PARTS * (parity + 1))
                                pool.tensor_tensor(w_lo[:, 1 - parity, ds(pair - 1, 1), :],
                                                   raw[:, 1 - parity, ds(pair - 1, 1), :],
                                                   f(w_hi[:, 1 - parity, ds(pair - 1, 1), :]),
                                                   ALU.subtract).then_inc(low_split, 1)

                pool.sem_inc(low_split, PARTS)
                walk(pool, body)


def moe_layer(nc, tag, psum, consts, dram, x, x_dram=None):
    with ExitStack() as ctx:
        sb = sb_in(ctx, nc)
        n_hi, n_lo = sb(f"{tag}_n_hi", [P, TOKENS], F32R), sb(f"{tag}_n_lo", [P, TOKENS], F32R)
        mask = sb(f"{tag}_mask", [P, TOKENS], F32R)
        w_hi = sb(f"{tag}_w_hi", [P, 2, PARTS, COLS], F32R)
        w_lo = sb(f"{tag}_w_lo", [P, 2, PARTS, COLS], F32R)
        with ExitStack() as small:
            names = ("router", "shared_gate", "shared_up", "shared_down")
            parts, splits = matrices(nc, small, tag, dram, names)
            first_group = [(dram[name][:, 0:COLS], w_hi[:, 0, m, :], w_lo[:, 0, m, :])
                           for m, name in enumerate(("gate", "up", "down"))]
            layernorm(nc, f"{tag}_norm", psum, consts, x, n_hi[:, :], n_lo[:, :], splits=splits + first_group,
                      x_dram=x_dram)
            route_and_share(nc, f"{tag}_route", psum, consts, parts["router"], [parts[name] for name in names[1:]],
                            n_hi, n_lo, mask, x)
        experts(nc, f"{tag}_experts", psum, consts, [dram[name] for name in ("gate", "up", "down")],
                w_hi, w_lo, n_hi, n_lo, mask, x)


TRAIL = 5


def head_attention(nc, tag, psum, consts, dram, x):
    with ExitStack() as ctx:
        sb, sem = sb_in(ctx, nc), sems_in(ctx, nc, tag)
        w_hi, w_lo = sb(f"{tag}_w_hi", [P, HEADS * P], F32R), sb(f"{tag}_w_lo", [P, HEADS * P], F32R)
        row_pick = consts["row_pick"]
        high_dram = nc.dram_tensor(f"{tag}_high", (P, TOKENS), F32, kind="Internal").ap()
        low_dram = nc.dram_tensor(f"{tag}_low", (P, TOKENS), F32, kind="Internal").ap()
        with ExitStack() as first:
            sb_first = sb_in(first, nc)
            n_hi, n_lo = sb_first(f"{tag}_n_hi", [P, TOKENS], F32R), sb_first(f"{tag}_n_lo", [P, TOKENS], F32R)
            layernorm(nc, f"{tag}_norm", psum, consts, x, n_hi[:, :], n_lo[:, :],
                      splits=[(dram["head_w"], w_hi[:, :], w_lo[:, :])], copies=(high_dram, low_dram))

        left = sb(f"{tag}_left", [P, 2, T], F32R)
        right = sb(f"{tag}_right", [P, 2, T], F32R)
        row_hi, row_lo = sb(f"{tag}_row_hi", [P, 2, T], F32R), sb(f"{tag}_row_lo", [P, 2, T], F32R)
        v_hi, v_lo = sb(f"{tag}_v_hi", [P, 2, TILES, 2, P], F32R), sb(f"{tag}_v_lo", [P, 2, TILES, 2, P], F32R)
        e = sb(f"{tag}_e", [P, 4, T])
        e_hi, e_lo = sb(f"{tag}_e_hi", [P, TILES, T], F32R), sb(f"{tag}_e_lo", [P, TILES, T], F32R)
        half_sums = sb(f"{tag}_half_sums", [P, 2, HALVES, TILES])
        sums = sb(f"{tag}_sums", [P, TILES])
        inverse = sb(f"{tag}_inverse", [P, 2, 32])
        inverse_rows = sb(f"{tag}_inverse_rows", [2 * 32, P], F32R)
        scale = sb(f"{tag}_scale", [P, HALVES, BANK])
        scaled = sb(f"{tag}_scaled", [P, HALVES, BANK])
        SCORES, OUT, ROWS, VALUES = 0, 2, 6, 7

        quads_loaded = [sem("quads_even"), sem("quads_odd")]
        rows_loaded = [sem("rows_even"), sem("rows_odd")]
        scores_done, exp_done, e_high, low_even, low_odd = (
            sem("scores"), sem("exp"), sem("e_high"), sem("low_even"), sem("low_odd"))
        out_done, v_done, v_high, v_low = sem("out"), sem("v"), sem("v_high"), sem("v_low")
        inverse_ready, turned, rows_high, rows_ready = sem("inverse"), sem("turned"), sem("rows_high"), sem("rows")
        spread_done, scale_ready, scaled_ready, added = sem("spread"), sem("scale"), sem("scaled"), sem("added")
        passed, pe_passed, pool_passed, inverse_clear, sums_ready = sem("passed"), sem("pe_passed"), sem("pool_passed"), sem("inverse_clear"), sem("sums")
        QUAD_LOADS, ROW_LOADS = 8 * QUAD, 2
        VALUE_STEPS = (5, 7)
        ITERATIONS = BATCH * HEADS // (2 * QUAD)

        def walk(eng, step):
            def two_quads(it):
                for parity in range(2):
                    for j in range(QUAD):
                        for s in range(TILES):
                            step(it, parity, j, s)
            two_quads(0)
            with eng.Fori(1, ITERATIONS) as it:
                two_quads(it)

        def head(it, parity, j):
            return it * (2 * QUAD) + (parity * QUAD + j)

        def number(it, parity, j, s):
            return it * (2 * QUAD * TILES) + ((parity * QUAD + j) * TILES + s)

        def none_before(it, parity, j):
            return isinstance(it, int) and it == 0 and parity == 0 and j == 0

        def low_sem(s):
            return low_odd if s % 2 else low_even

        def low_count(it, parity, j, s):
            return it * (QUAD * TILES) + ((parity * QUAD + j) * TILES + s) // 2 + 1

        def piece(it, parity, j, s):
            return it * 16 + (parity * 8 + j * 2 + (s == VALUE_STEPS[1])) + 5

        with nc.Block() as block:
            @block.sync
            def _(sp):
                def load_rows(it, parity):
                    at = ds((it // 2) * T, T)
                    sp.dma_start(f(row_hi[:, parity, :]), high_dram[:, at]).then_inc(rows_loaded[parity], 16)
                    sp.dma_start(f(row_lo[:, parity, :]), low_dram[:, at]).then_inc(rows_loaded[parity], 16)

                def free(it, parity):
                    count = it * (2 * QUAD * TILES * HALVES) + (parity - 1) * (QUAD * TILES * HALVES)
                    if isinstance(count, int):
                        after(sp, scores_done, count)
                    else:
                        wait_apart(sp, scores_done, count, passed)

                def load(it, parity):
                    free(it, parity)
                    load_rows(it, parity)
                    at = ds((it // 2) * T, T)
                    for j in range(QUAD):
                        dims = ds((it % 2) * (2 * QUAD * HEAD) + (parity * QUAD + j) * HEAD, HEAD)
                        high, low = high_dram[dims, at], low_dram[dims, at]
                        for tile, sources in ((left, (high, low, high, low)), (right, (high, low, low, high))):
                            for i, source in enumerate(sources):
                                start = 32 * j + i * HEAD
                                sp.dma_start(f(tile[start:start + HEAD, parity, :]), source).then_inc(quads_loaded[parity], 16)

                for parity in range(2):
                    load(0, parity)
                with sp.Fori(1, ITERATIONS) as it:
                    for parity in range(2):
                        load(it, parity)
                free(ITERATIONS, 0)
                load_rows(0, 0)

            @block.tensor
            def _(pe):
                def values(it, parity, jp, piece_count, i, bank=VALUES, before=1):
                    after(pe, v_low, piece_count - before)
                    cols = ds((it % 2) * (2 * QUAD * P) + (parity * QUAD + jp * 2) * P, 2 * P)
                    for v in (2 * i, 2 * i + 1):
                        tile = slice(v * P, (v + 1) * P)
                        last = product(pe, psum[:, bank, (v % 2) * 2 * P:(v % 2 + 1) * 2 * P],
                                       (row_hi[:, parity, tile], row_lo[:, parity, tile]),
                                       (w_hi[:, cols], w_lo[:, cols]))
                    last.then_inc(v_done, 1)

                def step(it, parity, j, s, tail=False):
                    n = number(it, parity, j, s)
                    h = head(it, parity, j)
                    started = not (isinstance(n, int) and n < TRAIL) and not (tail and s >= TRAIL)
                    ps, pj = (s - TRAIL) % TILES, (j - (s < TRAIL)) % QUAD
                    if not tail and j == 0 and s == 0:
                        pe.wait_ge(quads_loaded[parity], it * (16 * QUAD_LOADS) + 16 * QUAD_LOADS)
                    for half in range(HALVES):
                        at = slice(half * BANK, (half + 1) * BANK)
                        if not tail:
                            rows = slice(32 * j, 32 * j + 32)
                            after(pe, exp_done, n * HALVES + (half - 1))
                            pe.matmul(psum[:, SCORES + half, :], left[rows, parity, s * P:(s + 1) * P],
                                      right[rows, parity, at], start=True, stop=True).then_inc(scores_done, 1)
                        if started:
                            if half == 0:
                                if ps == 0:
                                    after(pe, scaled_ready, (h - 1) * HALVES)
                                    if j % 2 == 0:
                                        pe.wait_ge(v_low, piece(it, parity, j, 0) - 1)
                                pe.wait_ge(low_sem(ps), low_count(it, parity, j, s - TRAIL))
                            v = (slice(None), (pj // 2) % 2, ps, pj % 2, slice(None))
                            last = product(pe, psum[:, OUT + HALVES * (pj % 2) + half, :], (v_hi[v], v_lo[v]),
                                           (e_hi[:, ps, at], e_lo[:, ps, at]), first=ps == 0, last=ps == TILES - 1)
                    if started:
                        last.then_inc(out_done, 1)
                    if not tail and s in VALUE_STEPS:
                        next_it = it + 1 if parity == 1 and j >= 2 else it
                        next_parity = (parity + (j >= 2)) % 2
                        if s == VALUE_STEPS[0] and j == 2:
                            pe.wait_ge(rows_loaded[next_parity], next_it * (16 * ROW_LOADS) + 16 * ROW_LOADS)
                        values(next_it, next_parity, (j // 2 + 1) % 2, piece(it, parity, j, s),
                               (j % 2) * 2 + VALUE_STEPS.index(s))
                    if none_before(it, parity, j):
                        return
                    if s == 1:
                        after(pe, scale_ready, (h - 1) * HALVES)
                        if isinstance(h, int):
                            pe.wait_ge(inverse_ready, h)
                        else:
                            wait_apart(pe, inverse_ready, h, pe_passed)
                        pe.transpose(psum[0:64, ROWS, 0:P], inverse[:, :, :].rearrange("p a b -> p (a b)"),
                                     consts["identity"]).then_inc(turned, 1)
                    if s in (3, 5):
                        half = (s - 3) // 2
                        pe.wait_ge(rows_ready, h)
                        if half:
                            pe.wait_ge(scale_ready, (h - 1) * HALVES + 1)
                        for q in range(4):
                            tile = half * 4 + q
                            last = pe.matmul(psum[:, ROWS, q * P:(q + 1) * P], row_pick(tile),
                                             inverse_rows[:, :], start=q == 0, stop=q == 3, skip_group_check=True)
                        last.then_inc(spread_done, 1)

                pe.wait_ge(rows_loaded[0], 16 * ROW_LOADS)
                for i in range(4):
                    values(0, 0, 0, i + 1, i, bank=VALUES - i % 2, before=2)
                walk(pe, step)
                for s in range(6):
                    step(ITERATIONS, 0, 0, s, tail=True)

            @block.scalar
            def _(act):
                def value_high(slot, i, count, pairs_done, bank=VALUES):
                    act.wait_ge(v_done, count)
                    after(act, out_done, pairs_done)
                    act.copy(v_hi[:, slot, 2 * i:2 * i + 2, :, :].rearrange("p a b c -> p (a b c)"),
                             psum[:, bank, :]).then_inc(v_high, 1)

                def step(it, parity, j, s, tail=False):
                    n = number(it, parity, j, s)
                    h = head(it, parity, j)
                    if not tail:
                        for half in range(HALVES):
                            act.wait_ge(scores_done, n * HALVES + (half + 1))
                            if half == 0:
                                after(act, low_sem(s), low_count(it, parity, j, s) - 2)
                            act.activation(e[:, s % 4, half * BANK:(half + 1) * BANK], psum[:, SCORES + half, :],
                                           ACT.Exp, scale=HEAD ** -0.5,
                                           accum_out=half_sums[:, j % 2, half, s:s + 1]).then_inc(exp_done, 1)
                    if s in VALUE_STEPS and not tail:
                        value_high((j // 2 + 1) % 2, (j % 2) * 2 + VALUE_STEPS.index(s), piece(it, parity, j, s),
                                   it * (2 * QUAD * TILES) + (parity * QUAD + (j // 2) * 2) * TILES)
                    if s in (4, 6) and not none_before(it, parity, j):
                        half = (s - 4) // 2
                        act.wait_ge(spread_done, (h - 1) * HALVES + (half + 1))
                        after(act, scaled_ready, (h - 2) * HALVES + (half + 1))
                        act.copy(scale[:, half, :], psum[:, ROWS, :]).then_inc(scale_ready, 1)

                for i in range(4):
                    value_high(0, i, i + 1, 0, bank=VALUES - i % 2)
                walk(act, step)
                for s in (4, 6):
                    step(ITERATIONS, 0, 0, s, tail=True)

            @block.vector
            def _(dve):
                def value_low(slot, i, count, bank=VALUES):
                    dve.wait_ge(v_high, count)
                    at = v_lo[:, slot, 2 * i:2 * i + 2, :, :].rearrange("p a b c -> p (a b c)")
                    high = v_hi[:, slot, 2 * i:2 * i + 2, :, :].rearrange("p a b c -> p (a b c)")
                    dve.tensor_tensor(at, psum[:, bank, :], f(high), ALU.subtract).then_inc(v_low, 1)

                def step(it, parity, j, s, tail=False):
                    n = number(it, parity, j, s)
                    h = head(it, parity, j)
                    before = not none_before(it, parity, j)
                    if s == 0 and before:
                        dve.wait_ge(exp_done, n * HALVES)
                        after(dve, turned, h - 1)
                        dve.tensor_tensor(sums[:, :], half_sums[:, (j - 1) % 2, 0, :], half_sums[:, (j - 1) % 2, 1, :],
                                          ALU.add).then_inc(sums_ready, 1)
                        dve.wait_ge(sums_ready, h)
                        dve.reciprocal(inverse[:, :, 0:TILES],
                                       sums[:, :].unsqueeze(1).to_broadcast([P, 2, TILES])).then_inc(inverse_ready, 1)
                    if not tail:
                        dve.wait_ge(exp_done, n * HALVES + HALVES)
                        after(dve, out_done, n - (TILES - 1))
                        dve.tensor_copy(e_hi[:, s, :], e[:, s % 4, :]).then_inc(e_high, 1)
                        if s % 2:
                            dve.wait_ge(e_high, n + 1)
                            dve.tensor_tensor(e_lo[:, s, :], e[:, s % 4, :], f(e_hi[:, s, :]),
                                              ALU.subtract).then_inc(low_odd, 1)
                    if s == 2 and before:
                        dve.wait_ge(turned, h)
                        after(dve, spread_done, (h - 1) * HALVES)
                        dve.tensor_copy(inverse_rows[:, :], psum[0:64, ROWS, 0:P]).then_inc(rows_high, 1)
                        dve.wait_ge(rows_high, h)
                        dve.tensor_tensor(inverse_rows[32:64, :], psum[32:64, ROWS, 0:P], f(inverse_rows[32:64, :]),
                                          ALU.subtract).then_inc(rows_ready, 1)
                    if s in VALUE_STEPS and not tail:
                        value_low((j // 2 + 1) % 2, (j % 2) * 2 + VALUE_STEPS.index(s), piece(it, parity, j, s))
                    if s == 6 and before:
                        for half in range(HALVES):
                            dve.wait_ge(out_done, h * TILES)
                            dve.wait_ge(scale_ready, (h - 1) * HALVES + half + 1)
                            after(dve, added, (h - 2) * HALVES + half + 1)
                            dve.tensor_tensor(scaled[:, half, :], scale[:, half, :],
                                              psum[:, OUT + HALVES * ((j - 1) % 2) + half, :],
                                              ALU.mult).then_inc(scaled_ready, 1)

                dve.memset(inverse[:, :, :], 0.0).then_inc(inverse_clear, 1)
                dve.wait_ge(inverse_clear, 1)
                for i in range(4):
                    value_low(0, i, i + 1, bank=VALUES - i % 2)
                walk(dve, step)
                for s in (0, 2, 6):
                    step(ITERATIONS, 0, 0, s, tail=True)

            @block.gpsimd
            def _(pool):
                def step(it, parity, j, s, tail=False):
                    n = number(it, parity, j, s)
                    h = head(it, parity, j)
                    if s % 2 == 0 and not tail:
                        pool.wait_ge(e_high, n + 1)
                        pool.tensor_tensor(e_lo[:, s, :], e[:, s % 4, :], f(e_hi[:, s, :]),
                                           ALU.subtract).then_inc(low_even, 1)
                    if s == 7 and not none_before(it, parity, j):
                        row = it // 2
                        if parity == 0 and j == 0:
                            row = (it - 1) // 2
                        for half in range(HALVES):
                            at = ds(row * T + half * BANK, BANK)
                            wait_apart(pool, scaled_ready, (h - 1) * HALVES + half + 1, pool_passed)
                            pool.tensor_tensor(x[:, at], x[:, at], scaled[:, half, :], ALU.add).then_inc(added, 1)

                walk(pool, step)
                step(ITERATIONS, 0, 0, 7, tail=True)
                pool.wait_ge(added, BATCH * HEADS * HALVES)


def recurrent_layer(nc, tag, psum, consts, dram, x, out=None):
    columns = consts["columns"]
    with ExitStack() as ctx:
        sb, sem = sb_in(ctx, nc), sems_in(ctx, nc, tag)
        n_hi, n_lo = sb(f"{tag}_n_hi", [P, TOKENS], F32R), sb(f"{tag}_n_lo", [P, TOKENS], F32R)
        w, splits = matrices(nc, ctx, tag, dram, ("wf", "uf", "wi", "ui", "wc", "uc", "wo", "uo"))
        layernorm(nc, f"{tag}_norm", psum, consts, x, n_hi[:, :], n_lo[:, :], splits=splits)
        gates = sb(f"{tag}_gates", [P, HALVES, 3, BANK])
        kept = sb(f"{tag}_kept", [P, HALVES, BANK])
        new = sb(f"{tag}_new", [P, HALVES, BANK])
        cell = sb(f"{tag}_cell", [P, HALVES, BANK])
        c_hi, c_lo = sb(f"{tag}_c_hi", [P, HALVES, BANK], F32R), sb(f"{tag}_c_lo", [P, HALVES, BANK], F32R)
        h = sb(f"{tag}_h", [P, HALVES, BANK])
        sums_ready, gates_ready, kept_ready, new_ready = sem("sums"), sem("gates"), sem("kept"), sem("new")
        cell_ready, high_ready, low_ready = sem("cell"), sem("high"), sem("low")
        out_ready, h_ready, added = sem("out"), sem("h"), sem("added")
        stored = sem("stored")
        OUT = 6

        with nc.Block() as block:
            @block.sync
            def _(sp):
                if out is not None:
                    for n in range(BATCH * HALVES):
                        at = slice(n * BANK, (n + 1) * BANK)
                        sp.wait_ge(added, n + 1)
                        sp.dma_start(out[:, at], x[:, at]).then_inc(stored, 16)
                    sp.wait_ge(stored, 16 * BATCH * HALVES)

            @block.tensor
            def _(pe):
                GATES = (("wf", "uf"), ("wi", "ui"), ("wc", "uc"))

                def from_input(t):
                    for half in range(HALVES):
                        at = ds(t * T + half * BANK, BANK)
                        after(pe, gates_ready, t * (3 * HALVES) + (half - 1) * 3)
                        for gate, (wn, _) in enumerate(GATES):
                            product(pe, psum[:, half * 3 + gate, :], w[wn], (n_hi[:, at], n_lo[:, at]), last=False)

                def from_cell(t):
                    for half in range(HALVES):
                        pe.wait_ge(low_ready, t * HALVES + half + 1)
                        for gate, (_, un) in enumerate(GATES):
                            product(pe, psum[:, half * 3 + gate, :], w[un], (c_hi[:, half, :], c_lo[:, half, :]),
                                    first=False).then_inc(sums_ready, 1)

                from_input(0)
                with pe.Fori(0, BATCH - 1) as t:
                    from_cell(t)
                    from_input(t + 1)
                from_cell(BATCH - 1)
                for n in range(BATCH * HALVES):
                    half, bank, at = n % HALVES, OUT + n % 2, slice(n * BANK, (n + 1) * BANK)
                    after(pe, h_ready, n - 1)
                    product(pe, psum[:, bank, :], w["wo"], (n_hi[:, at], n_lo[:, at]), last=False)
                    if n < HALVES:
                        pe.wait_ge(low_ready, BATCH * HALVES + half + 1)
                    product(pe, psum[:, bank, :], w["uo"], (c_hi[:, half, :], c_lo[:, half, :]),
                            first=False).then_inc(out_ready, 1)

            @block.scalar
            def _(act):
                act.wait_ge(cell_ready, HALVES)
                for half in range(HALVES):
                    act.copy(c_hi[:, half, :], cell[:, half, :]).then_inc(high_ready, 1)
                with act.Fori(0, BATCH) as t:
                    for half in range(HALVES):
                        for gate, (func, bias) in enumerate(((ACT.Sigmoid, "bf"), (ACT.Sigmoid, "bi"), (ACT.Tanh, "bc"))):
                            act.wait_ge(sums_ready, t * (3 * HALVES) + half * 3 + gate + 1)
                            act.activation(gates[:, half, gate, :], psum[:, half * 3 + gate, :], func,
                                           bias=columns[bias]).then_inc(gates_ready, 1)
                    for half in range(HALVES):
                        act.wait_ge(cell_ready, t * HALVES + HALVES + half + 1)
                        act.copy(c_hi[:, half, :], cell[:, half, :]).then_inc(high_ready, 1)
                for n in range(BATCH * HALVES):
                    act.wait_ge(out_ready, n + 1)
                    after(act, added, n - 1)
                    act.activation(h[:, n % 2, :], psum[:, OUT + n % 2, :], ACT.Tanh, bias=columns["bo"]).then_inc(h_ready, 1)

            @block.vector
            def _(dve):
                for half in range(HALVES):
                    dve.tensor_copy(cell[:, half, :], columns["in_c"].to_broadcast([P, BANK])).then_inc(cell_ready, 1)
                for half in range(HALVES):
                    dve.wait_ge(high_ready, half + 1)
                    dve.tensor_tensor(c_lo[:, half, :], cell[:, half, :], f(c_hi[:, half, :]), ALU.subtract).then_inc(low_ready, 1)
                with dve.Fori(0, BATCH) as t:
                    for half in range(HALVES):
                        dve.wait_ge(gates_ready, t * (3 * HALVES) + half * 3 + 3)
                        dve.wait_ge(low_ready, t * HALVES + HALVES)
                        dve.tensor_tensor(kept[:, half, :], gates[:, half, 0, :], cell[:, half, :], ALU.mult).then_inc(kept_ready, 1)
                        dve.tensor_tensor(new[:, half, :], gates[:, half, 1, :], gates[:, half, 2, :], ALU.mult).then_inc(new_ready, 1)
                        dve.wait_ge(kept_ready, t * HALVES + half + 1)
                        dve.wait_ge(new_ready, t * HALVES + half + 1)
                        dve.tensor_tensor(cell[:, half, :], kept[:, half, :], new[:, half, :], ALU.add).then_inc(cell_ready, 1)
                    for half in range(HALVES):
                        dve.wait_ge(high_ready, t * HALVES + HALVES + half + 1)
                        dve.tensor_tensor(c_lo[:, half, :], cell[:, half, :], f(c_hi[:, half, :]), ALU.subtract).then_inc(low_ready, 1)
                for n in range(BATCH * HALVES):
                    at = slice(n * BANK, (n + 1) * BANK)
                    dve.wait_ge(h_ready, n + 1)
                    dve.scalar_tensor_tensor(out=x[:, at], in0=h[:, n % 2, :], scalar=0.5, in1=x[:, at],
                                             op0=ALU.mult, op1=ALU.add).then_inc(added, 1)
                dve.wait_ge(added, BATCH * HALVES)


def decayed_attention(nc, tag, psum, consts, w, tables, xn, residual):
    columns, inv, causal, ones = consts["columns"], consts["inv"], consts["causal"], consts["ones"]
    (n_hi, n_lo), (cosines, sines) = xn, tables
    with ExitStack() as ctx:
        sb, sem = sb_in(ctx, nc), sems_in(ctx, nc, tag)
        row_hi, row_lo = sb(f"{tag}_row_hi", [P, T], F32R), sb(f"{tag}_row_lo", [P, T], F32R)
        names = ("decay", "decay_log", "decay_max", "clock", "clock_log", "clock_max", "logit", "gain",
                 "total", "q_rotated", "q_swapped", "q_norm")
        tile = {name: sb(f"{tag}_{name}", [P, T])[:, :] for name in names}
        q, k, v = ([sb(f"{tag}_{name}_{part}", [P, T], F32R) for part in ("hi", "lo")] for name in "qkv")
        e = [tile[name] for name in ("decay_log", "decay_max", "clock")]
        inverse, out = (tile[name].rearrange("p (a b) -> p a b", a=HALVES) for name in ("gain", "total"))
        with ExitStack() as shared:
            tile |= {name: sb_in(shared, nc)(f"{tag}_{name}", [P, T])[:, :] for name in ("k_rotated", "k_swapped", "k_norm")}
        e_hi, e_lo = sb(f"{tag}_e_hi", [P, 3, T], F32R), sb(f"{tag}_e_lo", [P, 3, T], F32R)
        top = sb(f"{tag}_top", [P, 1])[:, :]
        products = {name: sem(f"p_{name}") for name in ("gate", "logit", "clock", "q", "q_swap", "q_square",
                                                        "k", "k_swap", "k_square", "v")}
        rows_loaded, sp_passed = sem("rows_loaded"), sem("sp_passed")
        abs_ready, exp_ready, log_ready, max_ready = ({kind: sem(f"{step}_{kind}") for kind in ("decay", "clock")}
                                                      for step in ("abs", "exp", "log", "max"))
        decay_sum, decay_clipped, decay_ready, clock_ready = sem("decay_sum"), sem("decay_clipped"), sem("decay"), sem("clock")
        logit_ready, top_ready, gain_exp, gain_ready, total_ready = (
            sem("logit"), sem("top"), sem("gain_exp"), sem("gain"), sem("total"))
        per_side = ("square", "norm_root", "norm_floor", "norm", "norm_inverse", "cosine", "sine", "rotated", "weighted", "ready", "high", "low")
        side = {name: {step: sem(f"{name}_{step}") for step in per_side} for name in ("q", "k")}
        v_high, v_low = sem("v_high"), sem("v_low")
        GATE, CLOCK, LOGIT, QUERY = 0, 2, 4, 6
        VALUES = LOGIT

        def pair(base):
            return psum[:, base:base + 2, :].rearrange("p a b -> p (a b)")

        banks = {"q": (QUERY, GATE, LOGIT), "k": (CLOCK, GATE, QUERY)}

        scores_done, masked, exp_done, e_high, e_low = sem("scores"), sem("masked"), sem("exp"), sem("e_high"), sem("e_low")
        out_done, inverse_ready, out_ready, added = sem("out_done"), sem("inverse"), sem("out"), sem("added")
        SCORES, OUT, SUMS = 0, 4, 6
        PIECES = BANK // P
        LATE = 2

        def segments(s):
            first = s * P
            return [(half, max(first - half * BANK, 0), BANK) for half in range(HALVES) if first < (half + 1) * BANK]

        def projected(eng, b):
            for s in (side["q"]["low"], side["k"]["low"], v_low):
                eng.wait_ge(s, b + 1)

        def rows(eng, prepare, attend):
            prepare(0)
            with eng.Fori(0, BATCH - 1) as b:
                attend(b)
                prepare(b + 1)
            attend(BATCH - 1)

        with nc.Block() as block:
            @block.sync
            def _(sp):
                def load(b):
                    sp.dma_start(f(row_hi[:, :]), f(n_hi[:, ds(b * T, T)])).then_inc(rows_loaded, 16)
                    sp.dma_start(f(row_lo[:, :]), f(n_lo[:, ds(b * T, T)])).then_inc(rows_loaded, 16)

                load(0)
                with sp.Fori(1, BATCH) as b:
                    wait_apart(sp, products["v"], b, sp_passed)
                    load(b)

            @block.tensor
            def _(pe):
                def project(b, name, base):
                    for half in range(HALVES):
                        at = ds(b * T + half * BANK, BANK)
                        last = product(pe, psum[:, base + half, :], w[name], (n_hi[:, at], n_lo[:, at]))
                    last.then_inc(products[name], 1)

                def square(b, name):
                    pe.wait_ge(side[name]["square"], b + 1)
                    for half in range(HALVES):
                        last = pe.matmul(psum[:, banks[name][2] + half, :], inv,
                                         tile[f"{name}_norm"][:, half * BANK:(half + 1) * BANK], start=True, stop=True)
                    last.then_inc(products[f"{name}_square"], 1)

                def prepare(b):
                    project(b, "gate", GATE)
                    project(b, "clock", CLOCK)
                    after(pe, inverse_ready, b * (HALVES * PIECES))
                    after(pe, out_ready, b * HALVES)

                def attend(b):
                    project(b, "logit", LOGIT)
                    project(b, "q", QUERY)
                    pe.wait_ge(max_ready["clock"], b + 1)
                    pe.wait_ge(abs_ready["clock"], b + 1)
                    project(b, "k", CLOCK)
                    pe.wait_ge(max_ready["decay"], b + 1)
                    pe.wait_ge(abs_ready["decay"], b + 1)
                    project(b, "q_swap", GATE)
                    pe.wait_ge(logit_ready, b + 1)
                    square(b, "q")
                    pe.wait_ge(side["q"]["cosine"], b + 1)
                    square(b, "k")
                    pe.wait_ge(side["q"]["sine"], b + 1)
                    project(b, "k_swap", GATE)
                    pe.wait_ge(side["q"]["norm_root"], b + 1)
                    pe.wait_ge(rows_loaded, b * 32 + 32)
                    for s in range(TILES):
                        at = slice(s * P, (s + 1) * P)
                        last = product(pe, psum[:, VALUES + s // 4, (s % 4) * P:(s % 4 + 1) * P],
                                       (row_hi[:, at], row_lo[:, at]), w["v_out"])
                    last.then_inc(products["v"], 1)
                    projected(pe, b)

                    for s in range(TILES + LATE):
                        if s < TILES:
                            at = slice(s * P, (s + 1) * P)
                            if s >= 2:
                                pe.wait_ge(exp_done, b * TILES + (s - 1))
                            for half, first, end in segments(s):
                                queries = slice(half * BANK + first, half * BANK + end)
                                last = product(pe, psum[:, SCORES + 2 * (s % 2) + half, first:end],
                                               (k[0][:, at], k[1][:, at]), (q[0][:, queries], q[1][:, queries]))
                            last.then_inc(scores_done, 1)
                        if s >= LATE:
                            p = s - LATE
                            at = slice(p * P, (p + 1) * P)
                            pe.wait_ge(e_low, b * TILES + (p + 1))
                            for half, first, end in segments(p):
                                cols = slice(half * BANK + first, half * BANK + end)
                                final = p == (half + 1) * (TILES // HALVES) - 1
                                product(pe, psum[:, OUT + half, first:end], (v[0][:, at], v[1][:, at]),
                                        (e_hi[:, p % 3, cols], e_lo[:, p % 3, cols]), first=p == 0, last=final)
                                pe.matmul(psum[:, SUMS + half, first:end], ones, e_lo[:, p % 3, cols],
                                          start=p == 0, stop=False, skip_group_check=True)
                                last = pe.matmul(psum[:, SUMS + half, first:end], ones, e_hi[:, p % 3, cols],
                                                 start=False, stop=final, skip_group_check=True)
                            last.then_inc(out_done, 1)

                rows(pe, prepare, attend)

            @block.scalar
            def _(act):
                KINDS = (("decay", GATE, "gate_b"), ("clock", CLOCK, "clock_b"))

                def prepare(b):
                    after(act, e_low, b * TILES)
                    after(act, out_done, b * TILES)
                    for kind, base, bias in KINDS:
                        act.wait_ge(products["gate" if kind == "decay" else "clock"], b + 1)
                        act.activation(tile[kind], pair(base), ACT.Abs, bias=columns[bias]).then_inc(abs_ready[kind], 1)
                    for kind, base, bias in KINDS:
                        act.wait_ge(abs_ready[kind], b + 1)
                        act.activation(tile[kind], tile[kind], ACT.Exp, scale=-1.0).then_inc(exp_ready[kind], 1)
                    for kind, base, bias in KINDS:
                        act.wait_ge(exp_ready[kind], b + 1)
                        act.activation(tile[f"{kind}_log"], tile[kind], ACT.Ln, bias=columns["one"]).then_inc(log_ready[kind], 1)

                def attend(b):
                    def square(name):
                        act.wait_ge(products[name], b + 1)
                        act.activation(tile[f"{name}_norm"], pair(banks[name][0]), ACT.Square).then_inc(side[name]["square"], 1)

                    def norm(name):
                        act.wait_ge(products[f"{name}_square"], b + 1)
                        act.activation(tile[f"{name}_norm"], pair(banks[name][2]), ACT.Sqrt,
                                       scale=float(P)).then_inc(side[name]["norm_root"], 1)

                    def high(name, target):
                        act.wait_ge(side[name]["ready"], b + 1)
                        act.copy(target[0][:, :], tile[f"{name}_rotated"]).then_inc(side[name]["high"], 1)

                    square("q")
                    square("k")
                    act.wait_ge(top_ready, b + 1)
                    act.activation(tile["gain"], tile["logit"], ACT.Exp, bias=top).then_inc(gain_exp, 1)
                    act.wait_ge(decay_clipped, b + 1)
                    act.activation(tile["decay"], tile["decay"], ACT.Exp, scale=-1.0).then_inc(decay_ready, 1)
                    norm("q")
                    norm("k")
                    act.wait_ge(products["v"], b + 1)
                    act.copy(v[0][:, :], pair(VALUES)).then_inc(v_high, 1)
                    high("q", q)
                    high("k", k)

                    for s in range(TILES):
                        first = s * P
                        act.wait_ge(masked, b * TILES + (s + 1))
                        if s >= 3:
                            act.wait_ge(e_low, b * TILES + (s - 2))
                        wide = psum[:, SCORES + 2 * (s % 2):SCORES + 2 * (s % 2) + 2, :].rearrange("p a b -> p (a b)")
                        act.activation(e[s % 3][:, first:T], wide[:, first:T], ACT.Exp, scale=float(P) ** -0.5).then_inc(exp_done, 1)
                        act.wait_ge(exp_done, b * TILES + (s + 1))
                        if s >= 3:
                            act.wait_ge(out_done, b * TILES + (s - 2))
                        act.copy(e_hi[:, s % 3, first:T], e[s % 3][:, first:T]).then_inc(e_high, 1)

                rows(act, prepare, attend)

            @block.vector
            def _(dve):
                def prepare(b):
                    for kind, base, bias in (("decay", GATE, "gate_b"), ("clock", CLOCK, "clock_b")):
                        dve.wait_ge(products["gate" if kind == "decay" else "clock"], b + 1)
                        dve.wait_ge(abs_ready[kind], b + 1)
                        dve.tensor_scalar(tile[f"{kind}_max"], pair(base), columns[bias], 0.0, ALU.add,
                                          ALU.max).then_inc(max_ready[kind], 1)
                    dve.wait_ge(log_ready["decay"], b + 1)
                    dve.wait_ge(max_ready["decay"], b + 1)
                    dve.tensor_tensor_scan(tile["decay"], tile["decay_max"], tile["decay_log"], 0.0,
                                           ALU.add, ALU.add).then_inc(decay_sum, 1)
                    dve.wait_ge(decay_sum, b + 1)
                    dve.tensor_scalar(tile["decay"], tile["decay"], 60.0, -50.0, ALU.min, ALU.max).then_inc(decay_clipped, 1)

                def attend(b):
                    def cosine(name):
                        dve.wait_ge(side[name]["square"], b + 1)
                        dve.tensor_tensor(tile[f"{name}_rotated"], cosines, pair(banks[name][0]),
                                          ALU.mult).then_inc(side[name]["cosine"], 1)

                    def sine(name):
                        dve.wait_ge(products[f"{name}_swap"], b + 1)
                        dve.tensor_tensor(tile[f"{name}_swapped"], sines, pair(banks[name][1]),
                                          ALU.mult).then_inc(side[name]["sine"], 1)

                    def finish(name, denominator, factor):
                        s, norm, rotated = side[name], tile[f"{name}_norm"], tile[f"{name}_rotated"]
                        dve.wait_ge(s["norm_root"], b + 1)
                        dve.tensor_scalar(norm, norm, 1e-12, None, ALU.max).then_inc(s["norm_floor"], 1)
                        dve.wait_ge(s["norm_floor"], b + 1)
                        dve.scalar_tensor_tensor(out=norm, in0=tile[denominator], scalar=1e-8, in1=norm,
                                                 op0=ALU.add, op1=ALU.mult).then_inc(s["norm"], 1)
                        dve.wait_ge(s["norm"], b + 1)
                        dve.reciprocal(norm, norm).then_inc(s["norm_inverse"], 1)
                        dve.wait_ge(s["weighted"], b + 1)
                        dve.wait_ge(s["norm_inverse"], b + 1)
                        dve.tensor_tensor(rotated, rotated, norm, ALU.mult).then_inc(s["ready"], 1)

                    dve.wait_ge(products["logit"], b + 1)
                    dve.tensor_scalar(tile["logit"], pair(LOGIT), columns["p_b"], None, ALU.add).then_inc(logit_ready, 1)
                    cosine("q")
                    sine("q")
                    dve.wait_ge(logit_ready, b + 1)
                    dve.tensor_reduce(top, tile["logit"], mybir.AxisListType.X, ALU.max, negate=True).then_inc(top_ready, 1)
                    cosine("k")
                    sine("k")
                    dve.wait_ge(gain_exp, b + 1)
                    dve.wait_ge(clock_ready, b + 1)
                    dve.tensor_tensor(tile["gain"], tile["gain"], tile["clock"], ALU.mult).then_inc(gain_ready, 1)
                    dve.wait_ge(gain_ready, b + 1)
                    dve.tensor_tensor_scan(tile["total"], tile["gain"], tile["gain"], 0.0, ALU.add, ALU.max).then_inc(total_ready, 1)
                    dve.wait_ge(total_ready, b + 1)
                    dve.wait_ge(decay_ready, b + 1)
                    finish("q", "total", "decay")
                    finish("k", "decay", "gain")
                    dve.wait_ge(v_high, b + 1)
                    dve.tensor_tensor(v[1][:, :], pair(VALUES), f(v[0][:, :]), ALU.subtract).then_inc(v_low, 1)

                    def invert(half, piece):
                        cols = slice(piece * P, (piece + 1) * P)
                        dve.wait_ge(out_done, b * TILES + (half + 1) * (TILES // HALVES))
                        dve.reciprocal(inverse[:, half, cols], psum[:, SUMS + half, cols]).then_inc(inverse_ready, 1)

                    def leave(half):
                        at = ds(b * T + half * BANK, BANK)
                        dve.wait_ge(inverse_ready, (b * HALVES + half + 1) * PIECES)
                        dve.tensor_tensor(out[:, half, :], inverse[:, half, :], psum[:, OUT + half, :], ALU.mult).then_inc(out_ready, 1)
                        dve.wait_ge(out_ready, b * HALVES + half + 1)
                        dve.scalar_tensor_tensor(out=residual[:, at], in0=out[:, half, :], scalar=columns["out_b"],
                                                 in1=residual[:, at], op0=ALU.add, op1=ALU.add).then_inc(added, 1)

                    for s in range(TILES):
                        half, first = s // 4, (s % 4) * P
                        block_at = psum[:, SCORES + 2 * (s % 2) + half, first:first + P]
                        dve.wait_ge(scores_done, b * TILES + (s + 1))
                        dve.tensor_tensor(block_at, causal, block_at, ALU.add).then_inc(masked, 1)
                        if s >= TILES - 2:
                            first_piece = (s - (TILES - 2)) * 2
                            for piece in (first_piece, first_piece + 1):
                                invert(0, piece)
                    leave(0)
                    for piece in range(PIECES):
                        invert(1, piece)
                    leave(1)

                rows(dve, prepare, attend)
                dve.wait_ge(added, BATCH * HALVES)

            @block.gpsimd
            def _(pool):
                with pool.Fori(0, BATCH) as b:
                    def sum_rotated(name, factor):
                        rotated, s = tile[f"{name}_rotated"], side[name]
                        pool.wait_ge(s["cosine"], b + 1)
                        pool.wait_ge(s["sine"], b + 1)
                        pool.tensor_tensor(rotated, rotated, tile[f"{name}_swapped"], ALU.add).then_inc(s["rotated"], 1)
                        pool.wait_ge(gain_ready if factor == "gain" else decay_ready, b + 1)
                        pool.wait_ge(s["rotated"], b + 1)
                        pool.tensor_tensor(rotated, rotated, tile[factor], ALU.mult).then_inc(s["weighted"], 1)

                    def low(name, target):
                        pool.wait_ge(side[name]["high"], b + 1)
                        pool.tensor_tensor(target[1][:, :], tile[f"{name}_rotated"], f(target[0][:, :]),
                                           ALU.subtract).then_inc(side[name]["low"], 1)

                    pool.wait_ge(max_ready["clock"], b + 1)
                    pool.wait_ge(log_ready["clock"], b + 1)
                    pool.tensor_tensor(tile["clock"], tile["clock_max"], tile["clock_log"], ALU.add).then_inc(clock_ready, 1)
                    sum_rotated("q", "decay")
                    sum_rotated("k", "gain")
                    low("q", q)
                    low("k", k)

                    for s in range(TILES):
                        first = s * P
                        pool.wait_ge(e_high, b * TILES + (s + 1))
                        pool.tensor_tensor(e_lo[:, s % 3, first:T], e[s % 3][:, first:T], f(e_hi[:, s % 3, first:T]),
                                           ALU.subtract).then_inc(e_low, 1)


def mlp_layer(nc, tag, psum, consts, w, h_parts, residual, x):
    columns = consts["columns"]
    h_hi, h_lo = h_parts
    W = 4
    with ExitStack() as ctx:
        sb, sem = sb_in(ctx, nc), sems_in(ctx, nc, tag)
        g = sb(f"{tag}_g", [P, 2, W, BANK])
        g_hi, g_lo = sb(f"{tag}_g_hi", [P, 2, W, BANK], F32R), sb(f"{tag}_g_lo", [P, 2, W, BANK], F32R)
        y = sb(f"{tag}_y", [P, 2, BANK])
        up_ready, gelu_ready, high_ready, low_ready, down_ready = sem("up"), sem("gelu"), sem("high"), sem("low"), sem("down")
        y_ready, added = sem("y"), sem("added")

        def tokens(c):
            return ds(c * BANK, BANK)

        with nc.Block() as block:
            @block.tensor
            def _(pe):
                def up(c, j):
                    after(pe, y_ready, c - 1)
                    for m in range(W):
                        cols = slice(m * P, (m + 1) * P)
                        product(pe, psum[:, j * W + m, :], (w["w1"][0][:, cols], w["w1"][1][:, cols]),
                                (h_hi[:, tokens(c)], h_lo[:, tokens(c)])).then_inc(up_ready, 1)

                def step(c, j, last):
                    if not last:
                        up(c + 1, 1 - j)
                    pe.wait_ge(gelu_ready, c * W + W)
                    for m in range(W):
                        cols = slice(m * P, (m + 1) * P)
                        pe.wait_ge(low_ready, c * W + (m + 1))
                        product(pe, psum[:, j * W, :], (w["w2"][0][:, cols], w["w2"][1][:, cols]),
                                (g_hi[:, j, m, :], g_lo[:, j, m, :]), first=m == 0, last=m == W - 1).then_inc(down_ready, 1)

                up(0, 0)
                each_chunk(pe, step)

            @block.scalar
            def _(act):
                def step(c, j, last):
                    for m in range(W):
                        act.wait_ge(up_ready, c * W + (m + 1))
                        after(act, low_ready, (c - 2) * W + (m + 1))
                        after(act, down_ready, (c - 2) * W + (m + 1))
                        act.activation(g[:, j, m, :], psum[:, j * W + m, :], ACT.Gelu,
                                       bias=columns[f"b1_{m}"]).then_inc(gelu_ready, 1)
                        act.wait_ge(gelu_ready, c * W + (m + 1))
                        act.copy(g_hi[:, j, m, :], g[:, j, m, :]).then_inc(high_ready, 1)

                each_chunk(act, step)

            @block.vector
            def _(dve):
                def leave(c, j):
                    dve.wait_ge(down_ready, c * W + W)
                    after(dve, added, c - 1)
                    dve.scalar_tensor_tensor(out=y[:, j, :], in0=psum[:, j * W, :], scalar=columns["b2"],
                                             in1=residual[:, tokens(c)], op0=ALU.add, op1=ALU.add).then_inc(y_ready, 1)
                    dve.wait_ge(y_ready, c + 1)
                    dve.tensor_tensor(x[:, tokens(c)], x[:, tokens(c)], y[:, j, :], ALU.add).then_inc(added, 1)

                def step(c, j, last):
                    if not (isinstance(c, int) and c == 0):
                        leave(c - 1, 1 - j)
                    for m in range(W):
                        dve.wait_ge(high_ready, c * W + (m + 1))
                        dve.tensor_tensor(g_lo[:, j, m, :], g[:, j, m, :], f(g_hi[:, j, m, :]), ALU.subtract).then_inc(low_ready, 1)

                each_chunk(dve, step)
                leave(CHUNKS - 1, 1)
                dve.wait_ge(added, CHUNKS)


def fold_output(nc, tag, psum, w, v_out):
    with ExitStack() as ctx:
        sem = sems_in(ctx, nc, tag)
        ready, high_ready, low_ready = sem("ready"), sem("high"), sem("low")
        with nc.Block() as block:
            @block.tensor
            def _(pe):
                product(pe, psum[:, 0, 0:P], w["v_turned"], w["out"]).then_inc(ready, 1)

            @block.vector
            def _(dve):
                dve.wait_ge(ready, 1)
                dve.tensor_copy(v_out[0], psum[:, 0, 0:P]).then_inc(high_ready, 1)
                dve.wait_ge(high_ready, 1)
                dve.tensor_tensor(v_out[1], psum[:, 0, 0:P], f(v_out[0]), ALU.subtract).then_inc(low_ready, 1)
                dve.wait_ge(low_ready, 1)


def decayed_attention_layer(nc, tag, psum, consts, dram, x):
    columns = consts["columns"]
    with ExitStack() as ctx:
        sb = sb_in(ctx, nc)
        residual = sb(f"{tag}_residual", [P, TOKENS])
        layernorm(nc, f"{tag}_norm", psum, consts, x, None, None, keep=residual)
        with ExitStack() as attention:
            sb = sb_in(attention, nc)
            n_hi, n_lo = (sb(f"{tag}_n_{part}", [P, TOKENS], F32R) for part in ("hi", "lo"))
            names = ("gate", "logit", "clock", "q", "q_swap", "k", "k_swap", "v_turned", "out")
            w, splits = matrices(nc, attention, f"{tag}_w", {name: dram[f"attn_{name}"] for name in names}, names)
            w["v_out"] = tuple(sb(f"{tag}_v_out_{part}", [P, P], F32R)[:, :] for part in ("hi", "lo"))
            tables = [sb(f"{tag}_{name}", [P, T]) for name in ("cosines", "sines")]
            layernorm(nc, f"{tag}_norm1", psum, consts, residual, n_hi[:, :], n_lo[:, :],
                      affine=(columns["ln1_g"], columns["ln1_b"]), splits=splits,
                      loads=[(table[:, :], dram[name]) for table, name in zip(tables, ("cosines", "sines"))])
            fold_output(nc, f"{tag}_fold", psum, w, w["v_out"])
            decayed_attention(nc, f"{tag}_attend", psum, consts, w, [table[:, :] for table in tables],
                              (n_hi, n_lo), residual)
        h_hi, h_lo = (sb_in(ctx, nc)(f"{tag}_h_{part}", [P, TOKENS], F32R) for part in ("hi", "lo"))
        w, splits = matrices(nc, ctx, f"{tag}_mlp_w", dram, ("w1", "w2"))
        layernorm(nc, f"{tag}_norm2", psum, consts, residual, h_hi[:, :], h_lo[:, :],
                  affine=(columns["ln2_g"], columns["ln2_b"]), splits=splits)
        mlp_layer(nc, f"{tag}_mlp", psum, consts, w, (h_hi, h_lo), residual, x)


VECTORS = ("gate_b", "p_b", "out_b", "clock_b", "one", "ln1_g", "ln1_b", "ln2_g", "ln2_b", "b2",
           "b1_0", "b1_1", "b1_2", "b1_3", "bf", "bi", "bc", "bo", "in_c")


def build(nc, dram, out):
    with ExitStack() as ctx:
        sb = sb_in(ctx, nc)
        psum = ctx.enter_context(nc.psum_tensor("psum", [P, 8, BANK], F32))
        x = sb("x", [P, TOKENS])
        inv, identity, eps = sb("inv", [P, P]), sb("identity", [P, P]), sb("eps", [P, 1])
        row_columns = sb("row_columns", [2 * 32, 32], F32R)
        causal, ones = sb("causal", [P, P]), sb("ones", [P, P], F32R)
        expert_rows = sb("expert_rows", [P, EXPERTS + 2 * GROUP])
        vectors = sb("vectors", [P, len(VECTORS)])
        load_constants(nc, [(inv[:, :], dram["inv"]),
                            (identity[:, :], dram["identity"]), (eps[:, :], dram["eps"]),
                            (causal[:, :], dram["causal"]), (vectors[:, :], dram["vectors"]),
                            (expert_rows[:, :], dram["expert_rows"])],
                       [(dram["row_columns"], row_columns[:, :]), (dram["ones"], ones[:, :])])
        consts = {"inv": inv[:, :], "identity": identity[:, :], "eps": eps[:, :],
                  "row_pick": lambda c: row_columns[:, c:c + 1].to_broadcast([2 * 32, P]),
                  "expert_rows": expert_rows, "causal": causal[:, :], "ones": ones[:, :],
                  "columns": {name: vectors[:, i:i + 1] for i, name in enumerate(VECTORS)}}
        moe_layer(nc, "moe0", psum, consts, dram, x, x_dram=dram["x"])
        head_attention(nc, "heads", psum, consts, dram, x)
        moe_layer(nc, "moe1", psum, consts, dram, x)
        recurrent_layer(nc, "cell0", psum, consts, dram, x)
        decayed_attention_layer(nc, "decay", psum, consts, dram, x)
        recurrent_layer(nc, "cell1", psum, consts, dram, x, out=out)


def kernel(**inputs):
    import numpy as np
    import concourse.bacc as bacc
    from concourse.bass_utils import run_bass_kernel_spmd

    def given(name):
        return np.asarray(inputs[name])

    def twice(a, axis):
        return np.concatenate([a, a], axis=axis)

    experts_up = ("L0_ffn_expert_gate_k", "L0_ffn_expert_up_k")
    gate, up = (given(name).transpose(1, 0, 2).reshape(P, EXPERTS * HIDDEN) for name in experts_up)
    rates = np.exp(-np.arange(P // 2, dtype=np.float32) * np.float32(math.log(10000.0) / (P // 2)))
    angles = np.arange(T, dtype=np.float32)[None, :] * np.repeat(rates, 2)[:, None]
    signs = np.tile(np.float32([-1.0, 1.0]), P // 2)[:, None]
    swapped = np.arange(P) ^ 1
    key, query = np.arange(P)[:, None], np.arange(P)[None, :]
    attn = "L1_attn_"
    vectors = {
        "gate_b": given(attn + "gate_b"), "p_b": given(attn + "p_b"), "out_b": given(attn + "out_b"),
        "clock_b": np.broadcast_to(given(attn + "clock_b"), (P,)), "one": np.ones(P, np.float32),
        "ln1_g": given(attn + "ln1_g"), "ln1_b": given(attn + "ln1_b"),
        "ln2_g": given(attn + "ln2_g"), "ln2_b": given(attn + "ln2_b"), "b2": given(attn + "mlp_b2"),
        **{f"b1_{m}": given(attn + "mlp_b1")[m * P:(m + 1) * P] for m in range(4)},
        **{name: given("L1_ffn_" + name) for name in ("bf", "bi", "bc", "bo", "in_c")},
    }
    arrays = {
        "x": given("L0_attn_x").reshape(TOKENS, P).T,
        "inv": np.full((P, P), 1.0 / P, np.float32),
        "identity": np.eye(P, dtype=np.float32),
        "eps": np.full((P, 1), EPS, np.float32),
        "router": twice(given("L0_ffn_router_w"), 1),
        "shared_gate": twice(given("L0_ffn_shared_gate_w"), 1),
        "shared_up": twice(given("L0_ffn_shared_up_w"), 1),
        "shared_down": twice(given("L0_ffn_shared_down_w"), 0),
        "gate": gate,
        "up": up,
        "down": given("L0_ffn_expert_down_k").reshape(PAIRS, P, P).transpose(1, 0, 2).reshape(P, PAIRS * P),
        "expert_rows": twice(np.eye(EXPERTS, EXPERTS + 2 * GROUP, dtype=np.float32), 0),
        "head_w": given("L0_attn_weight").reshape(HEADS, P, P).transpose(1, 0, 2).reshape(P, HEADS * P),
        "row_columns": np.tile(np.eye(32, dtype=np.float32), (2, 1)),
        "causal": np.where(query >= key, 0.0, -1e37).astype(np.float32),
        "ones": np.ones((P, P), np.float32),
        "vectors": np.stack([vectors[name] for name in VECTORS], axis=1),
        "cosines": np.cos(angles),
        "sines": np.sin(angles) * signs,
        **{name: given("L1_ffn_" + name).T for name in ("wf", "uf", "wi", "ui", "wc", "uc", "wo", "uo")},
        "attn_gate": given(attn + "gate_W"),
        "attn_logit": given(attn + "p_W"),
        "attn_clock": np.broadcast_to(given(attn + "clock_W"), (P, P)),
        "attn_q": given(attn + "Wq"),
        "attn_q_swap": given(attn + "Wq")[:, swapped],
        "attn_k": given(attn + "Wk"),
        "attn_k_swap": given(attn + "Wk")[:, swapped],
        "attn_v_turned": given(attn + "Wv").T,
        "attn_out": given(attn + "out_W"),
        "w1": given(attn + "mlp_W1"),
        "w2": given(attn + "mlp_W2").reshape(4, P, P).transpose(1, 0, 2).reshape(P, 4 * P),
    }
    arrays = {name: np.ascontiguousarray(a) for name, a in arrays.items()}
    nc = bacc.Bacc("TRN2", target_bir_lowering=False, num_devices=1)
    dram = {name: nc.dram_tensor(f"in_{name}", a.shape, F32, kind="ExternalInput").ap() for name, a in arrays.items()}
    out = nc.dram_tensor("out", (P, TOKENS), F32, kind="ExternalOutput").ap()
    build(nc, dram, out)
    result = run_bass_kernel_spmd(nc, [{f"in_{name}": a for name, a in arrays.items()}], core_ids=[0])
    return result.results[0]["out"].T.reshape(BATCH, T, P)
```
